# Optimizing a Trainium2 kernel written in Bass

```python
import numpy as np
import jax
import jax.numpy as jnp

def _softmax(x, axis=-1):
    return jax.nn.softmax(x, axis=axis)

def _gelu(x):
    return jax.nn.gelu(x, approximate=True)

def _silu(x):
    return jax.nn.silu(x)

def _sigmoid(x):
    return jax.nn.sigmoid(x)

def _layernorm(x, axis=-1, eps=1e-05):
    m = jnp.mean(x, axis=axis, keepdims=True)
    v = jnp.var(x, axis=axis, keepdims=True)
    return (x - m) / jnp.sqrt(v + eps)

def _scatter_add(tgt, idx, src, axis=0):
    return tgt.at[idx].add(src)

def _segment_sum(src, seg, n):
    return jax.ops.segment_sum(src, seg, n)
kernel_name = 'mk_gnn_preln_d1_gnn_r8_5d2c8e'

def setup_inputs(seed: int=0):
    np.random.seed(seed)
    _w = jnp.asarray

    def _rec_inputs():
        import jax
        import jax.numpy as jnp
        _gk = jax.random.key(seed)
        x = -0.0006008 + 1.001 * jax.random.normal(jax.random.fold_in(_gk, 1), (6250, 256), jnp.float32)
        src = jax.random.randint(jax.random.fold_in(_gk, 2), (200000,), 0, 6250, jnp.int32)
        dst = jnp.minimum((6250 * jax.random.uniform(jax.random.fold_in(_gk, 3), (200000,)) ** 2.0).astype(jnp.int32), 49999)
        _o = jnp.argsort(dst, stable=True)
        src = src[_o]
        dst = dst[_o]
        edge_weight = -0.00278149 + 0.998712 * jax.random.normal(jax.random.fold_in(_gk, 12), (200000,), jnp.float32)
        return (x, src, dst, edge_weight)
    x, src, dst, edge_weight = _rec_inputs()

    def _L0_gnn_setup():
        import jax, jax.numpy as jnp
        import numpy as np
        N = 1250
        E = 40000
        D = 256
        EPS = 1e-05

        def layer_norm(x, g, b):
            mu = jnp.mean(x, axis=-1, keepdims=True)
            var = jnp.mean(jnp.square(x - mu), axis=-1, keepdims=True)
            return (x - mu) * jax.lax.rsqrt(var + EPS) * g + b

        def linear(x, w, b):
            return x @ w + b
        key = jax.random.key(seed)
        ks = jax.random.split(key, 20)
        s = 1.0 / np.sqrt(D)
        inp = {'x': jax.random.normal(ks[0], (N, D), jnp.float32), 'edge_index': jax.random.randint(ks[1], (2, E), 0, N, jnp.int64), 'edge_weight': jax.random.normal(ks[2], (E,), jnp.float32), 'wq': jax.random.normal(ks[3], (D, D), jnp.float32) * s, 'bq': jnp.zeros((D,), jnp.float32), 'wk': jax.random.normal(ks[4], (D, D), jnp.float32) * s, 'bk': jnp.zeros((D,), jnp.float32), 'wv': jax.random.normal(ks[5], (D, D), jnp.float32) * s, 'bv': jnp.zeros((D,), jnp.float32), 'ws': jax.random.normal(ks[6], (D, D), jnp.float32) * s, 'bs': jnp.zeros((D,), jnp.float32), 'we': jax.random.normal(ks[7], (1, 1), jnp.float32), 'be': jnp.zeros((1,), jnp.float32), 'g1': jnp.ones((D,), jnp.float32), 'b1': jnp.zeros((D,), jnp.float32), 'g2': jnp.ones((D,), jnp.float32), 'b2': jnp.zeros((D,), jnp.float32), 'w_ff1': jax.random.normal(ks[8], (D, 2 * D), jnp.float32) * s, 'b_ff1': jnp.zeros((2 * D,), jnp.float32), 'w_ff2': jax.random.normal(ks[9], (2 * D, D), jnp.float32) * (1.0 / np.sqrt(2 * D)), 'b_ff2': jnp.zeros((D,), jnp.float32)}
        return inp
    _L0_gnn_all = _L0_gnn_setup()
    _L0_gnn_in = {k: v for k, v in _L0_gnn_all.items() if k in ('wq', 'bq', 'wk', 'bk', 'wv', 'bv', 'ws', 'bs', 'we', 'be', 'g1', 'b1', 'g2', 'b2', 'w_ff1', 'b_ff1', 'w_ff2', 'b_ff2')}
    del _L0_gnn_all
    return {'x': x, 'src': src, 'dst': dst, 'edge_weight': edge_weight, 'L0_gnn_wq': _L0_gnn_in['wq'], 'L0_gnn_bq': _L0_gnn_in['bq'], 'L0_gnn_wk': _L0_gnn_in['wk'], 'L0_gnn_bk': _L0_gnn_in['bk'], 'L0_gnn_wv': _L0_gnn_in['wv'], 'L0_gnn_bv': _L0_gnn_in['bv'], 'L0_gnn_ws': _L0_gnn_in['ws'], 'L0_gnn_bs': _L0_gnn_in['bs'], 'L0_gnn_we': _L0_gnn_in['we'], 'L0_gnn_be': _L0_gnn_in['be'], 'L0_gnn_g1': _L0_gnn_in['g1'], 'L0_gnn_b1': _L0_gnn_in['b1'], 'L0_gnn_g2': _L0_gnn_in['g2'], 'L0_gnn_b2': _L0_gnn_in['b2'], 'L0_gnn_w_ff1': _L0_gnn_in['w_ff1'], 'L0_gnn_b_ff1': _L0_gnn_in['b_ff1'], 'L0_gnn_w_ff2': _L0_gnn_in['w_ff2'], 'L0_gnn_b_ff2': _L0_gnn_in['b_ff2']}

def reference(x, src, dst, edge_weight, L0_gnn_wq, L0_gnn_bq, L0_gnn_wk, L0_gnn_bk, L0_gnn_wv, L0_gnn_bv, L0_gnn_ws, L0_gnn_bs, L0_gnn_we, L0_gnn_be, L0_gnn_g1, L0_gnn_b1, L0_gnn_g2, L0_gnn_b2, L0_gnn_w_ff1, L0_gnn_b_ff1, L0_gnn_w_ff2, L0_gnn_b_ff2):
    import jax
    import jax.numpy as jnp

    def _L0_gnn_ref(x, edge_index, edge_weight, wq, bq, wk, bk, wv, bv, ws, bs, we, be, g1, b1, g2, b2, w_ff1, b_ff1, w_ff2, b_ff2):
        import jax, jax.numpy as jnp
        import numpy as np
        N = 1250
        E = 40000
        D = 256
        EPS = 1e-05

        def layer_norm(x, g, b):
            mu = jnp.mean(x, axis=-1, keepdims=True)
            var = jnp.mean(jnp.square(x - mu), axis=-1, keepdims=True)
            return (x - mu) * jax.lax.rsqrt(var + EPS) * g + b

        def linear(x, w, b):
            return x @ w + b
        n = x.shape[0]
        scale = x.shape[-1] ** (-0.5)
        q = linear(x, wq, bq)
        k = linear(x, wk, bk)
        v = linear(x, wv, bv)
        src, dst = (edge_index[0], edge_index[1])
        scores = jnp.sum(q[dst] * k[src], axis=-1) * scale
        scores = scores + (edge_weight[:, None] @ we + be)[:, 0]
        seg_max = jax.ops.segment_max(scores, dst, num_segments=n)
        exp_s = jnp.exp(scores - seg_max[dst])
        denom = jax.ops.segment_sum(exp_s, dst, num_segments=n)
        attn = exp_s / jnp.maximum(denom[dst], 1e-12)
        message = v[src] * attn[:, None]
        out = jax.ops.segment_sum(message, dst, num_segments=n)
        x = layer_norm(x + out + linear(x, ws, bs), g1, b1)
        ffn = linear(jax.nn.gelu(linear(x, w_ff1, b_ff1)), w_ff2, b_ff2)
        x = layer_norm(x + ffn, g2, b2)
        return x
    edge_index = jnp.stack([src, dst])
    h = jnp.maximum(_layernorm(x, axis=-1), 0.0)
    x = x + _L0_gnn_ref(h, edge_index, edge_weight, L0_gnn_wq, L0_gnn_bq, L0_gnn_wk, L0_gnn_bk, L0_gnn_wv, L0_gnn_bv, L0_gnn_ws, L0_gnn_bs, L0_gnn_we, L0_gnn_be, L0_gnn_g1, L0_gnn_b1, L0_gnn_g2, L0_gnn_b2, L0_gnn_w_ff1, L0_gnn_b_ff1, L0_gnn_w_ff2, L0_gnn_b_ff2)
    return x

_drawn_inputs = setup_inputs


def setup_inputs(seed=0):
    import zlib

    import numpy as np

    out = dict(_drawn_inputs(seed))
    spreads = {'L0_gnn_bq': (0.0, 0.8),
     'L0_gnn_bk': (0.0, 0.8),
     'L0_gnn_bv': (0.0, 0.1),
     'L0_gnn_bs': (0.0, 0.1),
     'L0_gnn_g1': (1.0, 0.2),
     'L0_gnn_b1': (0.0, 0.1),
     'L0_gnn_g2': (1.0, 0.2),
     'L0_gnn_b2': (0.0, 0.1),
     'L0_gnn_b_ff1': (0.0, 0.1),
     'L0_gnn_b_ff2': (0.0, 0.1)}
    factors = {'edge_weight': 8.0}
    for name, (base, spread) in spreads.items():
        noise = np.random.default_rng([zlib.crc32(name.encode()), seed]).standard_normal(out[name].shape)
        drawn = base * np.exp(spread * noise) if base else spread * noise
        out[name] = jnp.asarray(drawn.astype(out[name].dtype))
    for name, factor in factors.items():
        out[name] = (out[name] * factor).astype(out[name].dtype)
    return out
```

```python
from contextlib import ExitStack

import concourse.bass as bass
from concourse import mybir

F32 = mybir.dt.float32
BF16 = mybir.dt.bfloat16
I32 = mybir.dt.int32
ALU = mybir.AluOpType
ACT = mybir.ActivationFunctionType
AX_X = mybir.AxisListType.X

P = 128
J = 4
C = P * J
U = 4
BIG = 1e30
NO_MAX = 5e29
PAD_DST = 32767
FIRST = 16
EPS = 1e-5


def ceil_div(a, b):
    return -(-a // b)


def gnn_layer(nc, x, src, dst, edge_weight, wq, bq, wk, bk, wv, bv, ws, bs, we, be, g1, b1, g2, b2,
              w_ff1, b_ff1, w_ff2, b_ff2, out):
    N, D = x.shape
    E = src.shape[0]
    F = w_ff1.shape[1]
    DC, FC = D // P, F // P
    D1 = D + 1
    SCALE = float(D) ** -0.5
    FULL = N // P
    REST = N - FULL * P
    B = ceil_div(N, P)
    NB = B + 1
    T = ceil_div(E, C)
    EP = T * C
    assert D == 2 * P and NB % 2 == 0 and REST > 0 and FULL % 2 == 0 and E % 16 == 0
    PAD = EP - E + 16
    ALL_STEPS = ceil_div(T * B, U) * U
    STAIR_STEPS = ceil_div(T + B - 1, U) * U
    HEAD = min(STAIR_STEPS + 8, T * B)
    TAIL = ALL_STEPS + 8 - T * B
    LEN = FIRST + ALL_STEPS + 16
    TG = ceil_div(T, P)
    assert HEAD <= min(2 * T, 512)

    ctx = ExitStack()
    with ctx:
        def sb(name, shape, dt=F32):
            return ctx.enter_context(nc.sbuf_tensor(name, shape, dt))

        def sem(name):
            return ctx.enter_context(nc.semaphore(name))

        def dram(name, shape, dt=F32):
            return nc.dram_tensor(name, shape, dt).ap()

        h_rows = dram("h_rows", (NB * P, D))
        r_rows = dram("r_rows", (NB * P, D))
        src_pad = dram("src_pad", (1, EP + 16), I32)
        dst_pad = dram("dst_pad", (1, EP + 16), I32)
        ew_pad = dram("ew_pad", (1, EP + 16))
        step_chunk = dram("step_chunk", (1, LEN), I32)
        step_block = [dram(f"step_block{k}", (1, LEN), I32) for k in range(3)]

        acc = sb("acc", [P, NB, D1])
        q3 = sb("q3", [P, NB, 3, D1 + 1], BF16)
        ident = sb("ident", [P, P])
        ones = sb("ones", [P, P])
        onesb = sb("onesb", [P, 1], BF16)
        wv_sb = sb("wv_sb", [P, DC, D])
        w1_sb = sb("w1_sb", [P, DC, F])
        w2_sb = sb("w2_sb", [P, FC, D])
        bias_names = ["bs", "bv", "g1", "b1", "g2", "b2", "b_ff2"]
        bias = sb("bias", [P, len(bias_names), D])
        row_of = {n: bias[:, k, :] for k, n in enumerate(bias_names)}
        bff1_col = sb("bff1_col", [P, FC])
        wb = sb("wb", [P, 2])
        stats = sb("stats", [P, NB, 6])
        mean = sb("mean", [P, NB])
        rstd = sb("rstd", [P, NB])
        nmr = sb("nmr", [P, NB])
        tmp = sb("tmp", [P, NB])
        eps = sb("eps", [P, 1])
        node = sb("node", [P, NB])
        neg_max = sb("neg_max", [P, NB])
        n_trips = sb("n_trips", [1, 1], I32)
        idx = sb("idx", [P, U, J], I32)
        ew = sb("ew", [P, U, J])
        dstb = sb("dstb", [P, U, C], I32)
        onehot = sb("onehot", [P, 2, J, P], BF16)
        WORK = 8420
        work = sb("work", [P, WORK])

        used = [0]

        def part(n, dt=F32):
            used[0] += n
            assert used[0] <= WORK, used
            a = work[:, used[0] - n:used[0]]
            return a if dt == F32 else a.bitcast(dt)

        banks = [ctx.enter_context(nc.psum_tensor(f"bank{k}", [P, 512], F32)) for k in range(8)]

        used[0] = 0
        wq_sb = part(DC * D).rearrange("p (c n) -> p c n", c=DC)
        wk_sb = part(DC * D).rearrange("p (c n) -> p c n", c=DC)
        ws_sb = part(DC * D).rearrange("p (c n) -> p c n", c=DC)
        wqT = part(DC * D).rearrange("p (c n) -> p c n", c=DC)
        wkT = part(DC * D1).rearrange("p (c n) -> p c n", c=DC)
        wqk = part(DC * D1).rearrange("p (c n) -> p c n", c=DC)
        bq_col = part(DC)
        q_bias = part(D1)
        h_now = part(2 * D).rearrange("p (k n) -> p k n", k=2)
        hT = part(2 * D).rearrange("p (k n) -> p k n", k=2)
        qf = part(D1)
        q_rest = part(D1)
        r_mid = part(D)
        r_out = part(2 * D).rearrange("p (k n) -> p k n", k=2)
        srow = part(HEAD)
        stair_t, stair_b, all_t, all_b = (part(HEAD) for _ in range(4))
        spare = dstb[:].rearrange("p u n -> p (u n)")
        row_t, row_b = spare[:, 0:HEAD], spare[:, HEAD:2 * HEAD]
        before = spare[:, 2 * HEAD:2 * HEAD + TG * HEAD // 2].bitcast(BF16).rearrange("p (g s) -> p g s", g=TG)
        ends_i = part(TG, I32)
        chunk_i = part(TG, I32)
        chunk_f = part(TG)
        ends = part(TG)
        falls = part(1)
        is_sorted = part(1)
        trips_f = part(1)
        node_i = part(NB, I32)
        padding = part(PAD, I32)
        zeros_i = part(PAD, I32)
        tail_t = part(TAIL, I32)
        tail_b = part(TAIL, I32)
        q3f = q3[:].rearrange("p b k n -> p (b k n)")
        EDGES_P = EP // P
        early = sb("early", [P, 2 * EDGES_P], I32)
        dst_a, dst_b = early[:, 0:EDGES_P], early[:, EDGES_P:2 * EDGES_P]
        pair_t = sb("pair_t", [B, T], I32)
        pair_b = sb("pair_b", [B, T], I32)

        ident_set, consts = sem("ident_set"), sem("consts")
        x_in = [sem(f"x_in{k}") for k in range(4)]
        x_rest_in, x_zero = sem("x_rest_in"), sem("x_zero")
        w_in, late_in = sem("w_in"), sem("late_in")
        edges_in, check_in, ends_in = sem("edges_in"), sem("check_in"), sem("ends_in")
        wT_ready, wT_copied, wqk_ready, wqk_copied = sem("wT_ready"), sem("wT_copied"), sem("wqk_ready"), sem("wqk_copied")
        stats_done, ln_link, var_done, std_done, ln_done = (sem(n) for n in ("stats_done", "ln_link", "var_done", "std_done", "ln_done"))
        h_done, h_stored, h_copied = sem("h_done"), sem("h_stored"), sem("h_copied")
        hT_ready, hT_copied = sem("hT_ready"), sem("hT_copied")
        q_ready, qf_done, hi_done, rest_done, mid_done, lo_done = (sem(n) for n in ("q_ready", "qf_done", "hi_done", "rest_done", "mid_done", "lo_done"))
        hws_ready, r_half, r_done = sem("hws_ready"), sem("r_half"), sem("r_done")
        r_stored = [sem(f"r_stored{k}") for k in range(2)]
        pairs_set, pairs_out = sem("pairs_set"), sem("pairs_out")
        plan, counts_ready, plan_done, heads_out = sem("plan"), sem("counts_ready"), sem("plan_done"), sem("heads_out")
        cleared = sem("cleared")

        def columns(v, n):
            return v.rearrange("(c p) -> p c", p=P)

        def every(v):
            return v.rearrange("(a n) -> a n", a=1).to_broadcast((P, v.shape[0]))

        def layer_stats(dve, turn):
            n = [5 * turn + 1]

            def link(i):
                i.then_inc(ln_link, 1)
                n[0] += 1
                dve.wait_ge(ln_link, n[0])

            dve.wait_ge(stats_done, turn + 1)
            nc.vector.tensor_tensor(mean[:], stats[:, :, 1], stats[:, :, 4], ALU.add)
            link(nc.vector.tensor_tensor(tmp[:], stats[:, :, 1], stats[:, :, 4], ALU.subtract))
            nc.vector.tensor_tensor(rstd[:], stats[:, :, 2], stats[:, :, 5], ALU.add)
            link(nc.vector.tensor_tensor(tmp[:], tmp[:], tmp[:], ALU.mult))
            nc.vector.tensor_scalar(mean[:], mean[:], 0.5, None, ALU.mult)
            link(nc.vector.tensor_scalar(tmp[:], tmp[:], 0.25, None, ALU.mult))
            nc.vector.scalar_tensor_tensor(out=rstd[:], in0=rstd[:], scalar=1.0 / D, in1=tmp[:], op0=ALU.mult, op1=ALU.add).then_inc(var_done, 1)
            dve.wait_ge(std_done, turn + 1)
            link(nc.vector.reciprocal(rstd[:], tmp[:]))
            link(nc.vector.scalar_tensor_tensor(out=nmr[:], in0=mean[:], scalar=-1.0, in1=rstd[:], op0=ALU.mult, op1=ALU.mult))
            nc.vector.tensor_copy(tmp[:], nmr[:]).then_inc(ln_done, 1)

        XG = FULL // 4
        with nc.Block() as block:
            @block.sync
            def _(sp):
                for k in range(4):
                    sp.dma_start(acc[:, k * XG:(k + 1) * XG, 0:D],
                                 x[k * XG * P:(k + 1) * XG * P, :].rearrange("(b p) d -> p b d", p=P)).then_inc(x_in[k], 16)
                sp.wait_ge(x_zero, 1)
                sp.dma_start(acc[0:REST, FULL, 0:D], x[FULL * P:N, :]).then_inc(x_rest_in, 16)
                for a, b in ((src, src_pad), (dst, dst_pad), (edge_weight, ew_pad)):
                    sp.dma_start(b[0, 0:E].rearrange("(a n) -> a n", a=16), a.rearrange("(a n) -> a n", a=16)).then_inc(edges_in, 16)
                sp.wait_ge(consts, 1)
                for a, b in ((zeros_i, src_pad), (padding, dst_pad)):
                    sp.dma_start(b[0:1, E:E + PAD], a[0:1, :]).then_inc(edges_in, 16)
                sp.dma_start(ew_pad[0:1, E:E + PAD], zeros_i[0:1, :].bitcast(F32)).then_inc(edges_in, 16)
                sp.wait_ge(edges_in, 6 * 16)
                sp.dma_start(dst_a, dst_pad[0, 0:EP].rearrange("(p n) -> p n", p=P)).then_inc(check_in, 16)
                sp.dma_start(dst_b, dst_pad[0, 1:EP + 1].rearrange("(p n) -> p n", p=P)).then_inc(check_in, 16)
                sp.wait_ge(consts, 2)
                chunks = dst_pad[0, 0:EP].rearrange("(t c) -> t c", c=C)
                for g in range(TG):
                    n = min(P, T - g * P)
                    sp.dma_start(ends_i[0:n, g:g + 1], chunks[g * P:g * P + n, C - 1:C], allow_slow_non_contiguous=True).then_inc(ends_in, 16)
                sp.wait_ge(pairs_set, 1)
                for tab, first, pairs, tail in ((step_chunk, FIRST, pair_t, tail_t), *((step_block[k], FIRST - k, pair_b, tail_b) for k in range(3))):
                    sp.dma_start(tab[0, first:first + T * B].rearrange("(b t) -> b t", t=T), pairs[:, :]).then_inc(pairs_out, 16)
                    sp.dma_start(tab[0:1, first + T * B:first + T * B + TAIL], tail[0:1, :]).then_inc(pairs_out, 16)
                with sp.Fori(0, NB) as i:
                    sp.wait_ge(h_done, i + 1)
                    sp.dma_start(h_rows[bass.ds(i * P, P), :], acc[:, bass.ds(i, 1), 0:D]).then_inc(h_stored, 16)
                with sp.Fori(0, NB // 2) as i:
                    for k in range(2):
                        sp.wait_ge(r_done, i * 2 + (k + 1))
                        sp.dma_start(r_rows[bass.ds((i * 2 + k) * P, P), :], r_out[:, k, :]).then_inc(r_stored[k], 16)
                sp.wait_ge(plan_done, 1)
                sp.wait_ge(pairs_out, 8 * 16)
                sp.dma_start(step_chunk[0:1, FIRST:FIRST + HEAD], row_t[0:1, :]).then_inc(heads_out, 16)
                for k in range(3):
                    sp.dma_start(step_block[k][0:1, FIRST - k:FIRST - k + HEAD], row_b[0:1, :]).then_inc(heads_out, 16)
                for k in range(2):
                    sp.wait_ge(r_stored[k], 16 * (NB // 2))
                sp.wait_ge(h_stored, 16 * NB)
                sp.wait_ge(heads_out, 4 * 16)
                sp.wait_ge(late_in, 16 * 12)

            @block.gpsimd
            def _(pool):
                pool.memset(ident[:], 0.0).then_inc(ident_set, 1)
                pool.wait_ge(ident_set, 1)
                pool.affine_select(out=ident[:], in_=ident[:], compare_op=ALU.not_equal, fill=1.0, base=0,
                                   pattern=[[-1, P]], channel_multiplier=1).then_inc(ident_set, 1)
                pool.memset(zeros_i[0:1, :], 0)
                pool.memset(padding[0:1, :], PAD_DST).then_inc(consts, 1)
                pool.memset(ends_i, PAD_DST).then_inc(consts, 1)
                pool.memset(tail_t[0:1, :], 0)
                pool.memset(tail_b[0:1, :], B)
                pool.iota(pair_t[:, :], [[1, T]], base=0, channel_multiplier=0)
                pool.iota(pair_b[:, :], [[0, T]], base=0, channel_multiplier=1).then_inc(pairs_set, 1)
                pool.iota(row_t, [[1, HEAD]], base=0, channel_multiplier=0)
                pool.iota(chunk_i, [[P, TG]], base=0, channel_multiplier=1)
                pool.iota(node_i, [[P, NB]], base=0, channel_multiplier=1).then_inc(consts, 1)

                def copy_h(i, k):
                    pool.wait_ge(h_done, i + 1)
                    pool.wait_ge(ident_set, 2)
                    nc.gpsimd.tensor_copy(h_now[:, k, :], acc[:, bass.ds(i, 1), 0:D]).then_inc(h_copied, 1)

                copy_h(0, 0)
                copy_h(1, 1)
                with pool.Fori(1, NB // 2) as i:
                    for k in range(2):
                        pool.wait_ge(hT_ready, i * 2 + (k - 1))
                        copy_h(i * 2 + k, k)

            @block.scalar
            def _(act):
                for w, t in ((wq, wq_sb), (wk, wk_sb), (ws, ws_sb)):
                    act.dma_start(t, w.rearrange("(c p) n -> p c n", p=P)).then_inc(w_in, 16)
                with nc.allow_non_contiguous_dma("columns of two biases"):
                    act.dma_start(wkT[:, :, D], columns(bk, DC)).then_inc(w_in, 16)
                    act.dma_start(bq_col, columns(bq, DC)).then_inc(w_in, 16)
                    act.dma_start(bff1_col[:], columns(b_ff1, FC)).then_inc(late_in, 16)
                for n, v in zip(bias_names, (bs, bv, g1, b1, g2, b2, b_ff2)):
                    act.dma_start(row_of[n], every(v)).then_inc(w_in if n == "bs" else late_in, 16)
                act.dma_start(wb[:, 0:1], every(we.rearrange("a b -> (a b)"))).then_inc(late_in, 16)
                act.dma_start(wb[:, 1:2], every(be)).then_inc(late_in, 16)
                act.dma_start(wv_sb[:], wv.rearrange("(c p) n -> p c n", p=P)).then_inc(late_in, 16)
                act.dma_start(w1_sb[:], w_ff1.rearrange("(c p) n -> p c n", p=P)).then_inc(late_in, 16)
                act.dma_start(w2_sb[:], w_ff2.rearrange("(c p) n -> p c n", p=P)).then_inc(late_in, 16)
                act.wait_ge(var_done, 1)
                nc.scalar.activation(tmp[:], rstd[:], ACT.Sqrt, bias=eps[:, 0:1]).then_inc(std_done, 1)
                act.wait_ge(ln_done, 1)
                with act.Fori(0, NB) as i:
                    a = acc[:, bass.ds(i, 1), 0:D]
                    nc.scalar.activation(a, a, ACT.Relu, bias=nmr[:, bass.ds(i, 1)], scale=rstd[:, bass.ds(i, 1)]).then_inc(h_done, 1)
                with act.Fori(0, NB) as i:
                    act.wait_ge(qf_done, i + 1)
                    act.wait_ge(ln_done, 1)
                    nc.scalar.copy(q3[:, bass.ds(i, 1), 0, 0:D1], qf).then_inc(hi_done, 1)
                    act.wait_ge(rest_done, i + 1)
                    act.wait_ge(ln_done, 1)
                    nc.scalar.copy(q3[:, bass.ds(i, 1), 1, 0:D1], q_rest).then_inc(mid_done, 1)

            @block.vector
            def _(dve):
                nc.vector.memset(acc[:, FULL:NB, :], 0.0).then_inc(x_zero, 1)
                nc.vector.memset(eps[:], EPS)
                nc.vector.memset(ones[:], 1.0)
                nc.vector.memset(onesb[:], 1.0)
                nc.vector.memset(neg_max[:], NO_MAX).then_inc(ln_link, 1)
                for k in range(2 * DC):
                    dve.wait_ge(wT_ready, k + 1)
                    nc.vector.tensor_copy((wqT if k < DC else wkT)[:, k % DC, 0:D], banks[k][:, 0:D]).then_inc(wT_copied, 1)
                for k in range(4):
                    dve.wait_ge(x_in[k], 16)
                    with dve.Fori(k * XG, (k + 1) * XG) as i:
                        nc.vector.bn_stats(stats[:, bass.ds(i, 1), :], acc[:, bass.ds(i, 1), 0:D])
                dve.wait_ge(x_rest_in, 16)
                for i in range(FULL, NB):
                    last = nc.vector.bn_stats(stats[:, i, :], acc[:, i, 0:D])
                last.then_inc(stats_done, 1)
                layer_stats(dve, 0)
                for k in range(DC):
                    dve.wait_ge(wqk_ready, k + 1)
                    nc.vector.tensor_copy(wqk[:, k, :], banks[4 + k][:, 0:D1]).then_inc(wqk_copied, 1)
                dve.wait_ge(wqk_ready, DC + 1)
                nc.vector.tensor_copy(q_bias, banks[6][:, 0:D1]).then_inc(wqk_copied, 1)
                dve.wait_ge(wqk_copied, DC + 1)
                dve.wait_ge(w_in, 6 * 16)

                def copy_hT(i, k):
                    dve.wait_ge(hT_ready, i + 1)
                    nc.vector.tensor_copy(hT[:, k, :], banks[0][:, 0:D]).then_inc(hT_copied, 1)

                def split_q(i, k, more):
                    if more:
                        copy_hT(i + 1, 1 - k)
                    dve.wait_ge(q_ready, i + 1)
                    nc.vector.tensor_tensor(qf, banks[1 + k][:, 0:D1], q_bias, ALU.add).then_inc(qf_done, 1)
                    dve.wait_ge(hi_done, i + 1)
                    nc.vector.tensor_tensor(q_rest, qf, q3[:, bass.ds(i, 1), 0, 0:D1], ALU.subtract).then_inc(rest_done, 1)
                    dve.wait_ge(hws_ready, i + 1)
                    nc.vector.tensor_tensor(r_mid, banks[3 + k][:, 0:D], row_of["bs"], ALU.add).then_inc(r_half, 1)
                    dve.wait_ge(r_half, i + 1)
                    nc.vector.tensor_tensor(r_out[:, k, :], r_mid, acc[:, bass.ds(i, 1), 0:D], ALU.add).then_inc(r_done, 1)
                    dve.wait_ge(mid_done, i + 1)
                    nc.vector.tensor_tensor(q3[:, bass.ds(i, 1), 2, 0:D1], q_rest, q3[:, bass.ds(i, 1), 1, 0:D1], ALU.subtract).then_inc(lo_done, 1)

                copy_hT(0, 0)
                split_q(0, 0, True)
                split_q(1, 1, True)
                with dve.Fori(1, NB // 2 - 1) as i:
                    for k in range(2):
                        dve.wait_ge(r_stored[k], i * 16)
                        split_q(i * 2 + k, k, True)
                for k in range(2):
                    dve.wait_ge(r_stored[k], (NB // 2 - 1) * 16)
                    split_q(NB - 2 + k, k, k == 0)
                dve.wait_ge(consts, 3)
                nc.vector.tensor_copy(srow, row_t)
                nc.vector.tensor_copy(node[:], node_i)
                nc.vector.tensor_copy(chunk_f, chunk_i)
                dve.wait_ge(ends_in, TG * 16)
                nc.vector.tensor_scalar(ends_i, ends_i, 7, None, ALU.arith_shift_right).then_inc(plan, 1)
                dve.wait_ge(plan, 1)
                nc.vector.scalar_tensor_tensor(out=ends, in0=ends_i, scalar=float(B - 1), in1=chunk_f, op0=ALU.min, op1=ALU.add).then_inc(plan, 1)
                dve.wait_ge(plan, 2)
                for g in range(TG):
                    nc.vector.tensor_scalar(before[:, g, :], srow, ends[:, g:g + 1], None, ALU.is_gt)
                dve.wait_ge(check_in, 32)
                nc.vector.tensor_tensor(dst_a, dst_a, dst_b, ALU.is_gt).then_inc(plan, 1)
                dve.wait_ge(plan, 3)
                nc.vector.tensor_reduce(falls, dst_a, AX_X, ALU.add).then_inc(plan, 1)
                dve.wait_ge(counts_ready, 1)
                cnt, bad = banks[7][0:1, 0:HEAD], banks[6][0:1, 0:1]
                nc.vector.tensor_scalar(is_sorted[0:1, :], bad, 0.0, None, ALU.is_equal)
                nc.vector.tensor_scalar(stair_t[0:1, :], cnt, float(T - 1), None, ALU.min)
                nc.vector.tensor_scalar(all_b[0:1, :], srow[0:1, :], float(T), None, ALU.is_ge).then_inc(plan, 1)
                dve.wait_ge(plan, 5)
                nc.vector.tensor_tensor(stair_b[0:1, :], srow[0:1, :], stair_t[0:1, :], ALU.subtract)
                nc.vector.scalar_tensor_tensor(out=all_t[0:1, :], in0=all_b[0:1, :], scalar=-float(T), in1=srow[0:1, :], op0=ALU.mult, op1=ALU.add)
                nc.vector.tensor_scalar(trips_f[0:1, :], is_sorted[0:1, :], float((STAIR_STEPS - ALL_STEPS) // U), float(ALL_STEPS // U), ALU.mult, ALU.add).then_inc(plan, 1)
                dve.wait_ge(plan, 6)
                nc.vector.tensor_copy(n_trips[:], trips_f[0:1, :])
                nc.vector.tensor_tensor(stair_t[0:1, :], stair_t[0:1, :], all_t[0:1, :], ALU.subtract)
                nc.vector.scalar_tensor_tensor(out=stair_b[0:1, :], in0=stair_b[0:1, :], scalar=float(B), in1=all_b[0:1, :], op0=ALU.min, op1=ALU.subtract).then_inc(plan, 1)
                dve.wait_ge(plan, 7)
                nc.vector.scalar_tensor_tensor(out=row_t[0:1, :], in0=stair_t[0:1, :], scalar=is_sorted[0:1, 0:1], in1=all_t[0:1, :], op0=ALU.mult, op1=ALU.add)
                nc.vector.scalar_tensor_tensor(out=row_b[0:1, :], in0=stair_b[0:1, :], scalar=is_sorted[0:1, 0:1], in1=all_b[0:1, :], op0=ALU.mult, op1=ALU.add).then_inc(plan_done, 1)
                dve.wait_ge(h_stored, 16 * NB)
                nc.vector.memset(acc[:], 0.0).then_inc(cleared, 1)

            @block.tensor
            def _(pe):
                pe.wait_ge(ident_set, 2)
                pe.wait_ge(w_in, 6 * 16)
                for k in range(2 * DC):
                    w = wq_sb if k < DC else wk_sb
                    c = k % DC
                    for r in range(DC):
                        last = nc.tensor.transpose(banks[k][:, r * P:(r + 1) * P], w[:, r, c * P:(c + 1) * P], ident[:])
                    last.then_inc(wT_ready, 1)
                pe.wait_ge(wT_copied, 2 * DC)
                for r in range(DC):
                    for c in range(DC):
                        last = nc.tensor.matmul(banks[4 + r][:, 0:D1], wqT[:, c, r * P:(r + 1) * P], wkT[:, c, :], start=(c == 0), stop=(c == DC - 1))
                    last.then_inc(wqk_ready, 1)
                for c in range(DC):
                    last = nc.tensor.matmul(banks[6][:, 0:D1], bq_col[:, c:c + 1].broadcast_to([P, P]), wkT[:, c, :], start=(c == 0), stop=(c == DC - 1))
                last.then_inc(wqk_ready, 1)

                def transpose_h(i, k):
                    pe.wait_ge(h_copied, i + 1)
                    for c in range(DC):
                        last = nc.tensor.transpose(banks[0][:, c * P:(c + 1) * P], h_now[:, k, c * P:(c + 1) * P], ident[:])
                    last.then_inc(hT_ready, 1)

                def project(i, k, more):
                    pe.wait_ge(hT_copied, i + 1)
                    if more:
                        transpose_h(i + 1, 1 - k)
                    for c in range(DC):
                        last = nc.tensor.matmul(banks[1 + k][:, 0:D1], hT[:, k, c * P:(c + 1) * P], wqk[:, c, :], start=(c == 0), stop=(c == DC - 1))
                    last.then_inc(q_ready, 1)
                    for c in range(DC):
                        last = nc.tensor.matmul(banks[3 + k][:, 0:D], hT[:, k, c * P:(c + 1) * P], ws_sb[:, c, :], start=(c == 0), stop=(c == DC - 1))
                    last.then_inc(hws_ready, 1)

                transpose_h(0, 0)
                pe.wait_ge(wqk_copied, DC + 1)
                with pe.Fori(0, NB // 2 - 1) as i:
                    for k in range(2):
                        project(i * 2 + k, k, True)
                project(NB - 2, 0, True)
                project(NB - 1, 1, False)
                pe.wait_ge(plan, 4)
                pe.wait_ge(r_done, NB)
                for g in range(TG):
                    nc.tensor.matmul(banks[7][0:1, 0:HEAD], onesb[:], before[:, g, :], start=(g == 0), stop=(g == TG - 1))
                nc.tensor.matmul(banks[6][0:1, 0:1], falls, ones[:, 0:1], start=True, stop=True).then_inc(counts_ready, 1)

        used[0] = 0
        rows = part(U * J * D1).rearrange("p (u j n) -> p u j n", u=U, j=J)
        masked = part(C)
        probsT = part(C)
        probs = part(C).rearrange("p (j n) -> p j n", j=J)
        outside = part(C, BF16)[:, 0:2 * C].rearrange("p (k n) -> p k n", k=2)
        product = part(J * (D1 + 1) // 2, BF16).rearrange("p (j n) -> p j n", j=J)
        score = part(2 * J).rearrange("p (k j) -> p k j", k=2)
        ew_term = part(2 * J).rearrange("p (k j) -> p k j", k=2)
        old_max = part(1)
        new_max = part(1)
        max_step = part(1)
        decay = part(2)

        ones_set = sem("ones_set")
        idx_in = [sem(f"idx_in{u}") for u in range(U)]
        ew_in = [sem(f"ew_in{u}") for u in range(U)]
        dst_in = [sem(f"dst_in{u}") for u in range(U)]
        rows_in = [sem(f"rows_in{u}") for u in range(U)]
        onehot_done, outside_done, q_edges, scored = sem("onehot_done"), sem("outside_done"), sem("q_edges"), sem("scored")
        ew_done, spread, max_read, masked_done, max_kept, max_done = (sem(n) for n in ("ew_done", "spread", "max_read", "masked_done", "max_kept", "max_done"))
        exp_done, turned, probs_done, summed, added = (sem(n) for n in ("exp_done", "turned", "probs_done", "summed", "added"))

        with nc.Block() as block:
            def trips(eng):
                return eng.value_load(n_trips[0:1, 0:1], min_val=STAIR_STEPS // U, max_val=ALL_STEPS // U)

            def listed(eng, regs, table, i):
                eng.load(regs, table[0:1, bass.ds(i * U + FIRST, U)])
                top = T - 1 if table is step_chunk else B
                return [eng.snap(r, min_val=0, max_val=top) for r in regs]

            @block.sync
            def _(sp):
                n = trips(sp)
                regs = [sp.alloc_register(f"chunk{u}") for u in range(U)]

                def fetch(chunk, u):
                    at = chunk * C
                    sp.dma_start(idx[:, u, :], src_pad[0, bass.ds(at, C)].rearrange("(p j) -> p j", j=J)).then_inc(idx_in[u], 16)
                    sp.dma_start(dstb[:, u, :], dst_pad[0:1, bass.ds(at, C)].to_broadcast((P, C))).then_inc(dst_in[u], 16)
                    sp.dma_start(ew[:, u, :], ew_pad[0, bass.ds(at, C)].rearrange("(p j) -> p j", j=J)).then_inc(ew_in[u], 16)

                for u, chunk in enumerate(listed(sp, regs, step_chunk, 0)):
                    fetch(chunk, u)
                with sp.Fori(1, n + 1) as i:
                    for u, chunk in enumerate(listed(sp, regs, step_chunk, i)):
                        gathered, used_steps = sp.snap(i * (16 * J)), sp.snap((i - 1) * U + (u + 1))
                        sp.wait_ge(edges_in, 6 * 16)
                        sp.wait_ge(rows_in[u], gathered)
                        sp.wait_ge(onehot_done, used_steps)
                        sp.wait_ge(ew_done, used_steps)
                        fetch(chunk, u)
                landed = sp.to_reg(n * 16 + 16)
                sp.wait_ge(edges_in, 6 * 16)
                for u in range(U):
                    for s in (idx_in[u], dst_in[u], ew_in[u]):
                        sp.wait_ge(s, landed)

            @block.gpsimd
            def _(pool):
                n = trips(pool)

                def gather(i, u, wait_free):
                    landed, free = pool.to_reg(i * 16 + 16), pool.to_reg(i * U + (u + 1))
                    pool.wait_ge(h_stored, 16 * NB)
                    if wait_free:
                        pool.wait_ge(summed, free)
                    pool.wait_ge(idx_in[u], landed)
                    for j in range(J):
                        pool.indirect_dma_start(rows[:, u, j, 0:D], None, h_rows, bass.IndirectOffsetOnAxis(idx[:, u, j:j + 1], 0)).then_inc(rows_in[u], 16)

                for u in range(U):
                    gather(0, u, False)
                with pool.Fori(1, n) as i:
                    for u in range(U):
                        gather(i, u, True)
                gather(n, 0, True)
                pool.wait_ge(rows_in[0], n * (16 * J) + 16 * J)

            @block.tensor
            def _(pe):
                n = trips(pe)
                regs = [pe.alloc_register(f"next_block{u}") for u in range(U)]

                def expand_q(s, k, b):
                    pe.wait_ge(onehot_done, s + 1)
                    for j in range(J):
                        for c in range(3):
                            last = nc.tensor.matmul(banks[j][:, 0:D1], onehot[:, k, j, :], q3[:, bass.ds(b, 1), c, 0:D1], start=(c == 0), stop=(c == 2))
                    last.then_inc(q_edges, 1)

                first = pe.alloc_register("first_block")
                pe.load([first], step_block[0][0:1, FIRST:FIRST + 1])
                pe.sem_inc(summed, U)
                expand_q(0, 0, pe.snap(first, min_val=0, max_val=B))
                with pe.Fori(0, n) as i:
                    blocks = listed(pe, regs, step_block[1], i)
                    for u in range(U):
                        s, k = i * U + u, u % 2
                        pe.wait_ge(scored, s + 1)
                        for j in range(J):
                            last = nc.tensor.transpose(banks[4][:, j * P:(j + 1) * P], score[:, k, j:j + 1].broadcast_to([P, P]), ident[:])
                        last.then_inc(spread, 1)
                        expand_q(s + 1, 1 - k, blocks[u])
                        pe.wait_ge(exp_done, s + 1)
                        for j in range(J):
                            last = nc.tensor.transpose(banks[5 - j // 2][:, (j % 2) * P:(j % 2 + 1) * P], probsT[:, j * P:(j + 1) * P], ident[:])
                            if j % 2:
                                last.then_inc(turned, 1)
                        for j in range(J):
                            if j % 2 == 0:
                                pe.wait_ge(probs_done, s * 2 + (1 + j // 2))
                            last = nc.tensor.matmul(banks[6 + k][:, 0:D1], probs[:, j, :], rows[:, u, j, :], start=(j == 0), stop=(j == J - 1))
                        last.then_inc(summed, 1)

            @block.scalar
            def _(act):
                n = trips(act)

                def mask(s, k):
                    act.wait_ge(onehot_done, s + 1)
                    nc.scalar.activation(outside[:, k, :], onehot[:, k].rearrange("p j n -> p (j n)"), ACT.Copy, scale=BIG, bias=-BIG).then_inc(outside_done, 1)

                mask(0, 0)
                with act.Fori(0, n) as i:
                    for u in range(U):
                        s, k = i * U + u, u % 2
                        mask(s + 1, 1 - k)
                        act.wait_ge(max_done, s + 1)
                        nc.scalar.activation(decay[:, k:k + 1], max_step, ACT.Exp)
                        nc.scalar.activation(probsT, masked, ACT.Exp, bias=new_max, scale=-1.0).then_inc(exp_done, 1)
                        for half in range(2):
                            act.wait_ge(turned, s * 2 + (1 + half))
                            nc.scalar.copy(probs[:, 2 * half:2 * half + 2, :].rearrange("p j n -> p (j n)"), banks[5 - half][:, 0:2 * P]).then_inc(probs_done, 1)

            @block.vector
            def _(dve):
                n = trips(dve)
                regs = [dve.alloc_register(f"block{u}") for u in range(U)]
                ahead = [dve.alloc_register(f"ahead{u}") for u in range(U)]
                nc.vector.memset(rows[:, :, :, D:D1], 1.0).then_inc(ones_set, 1)

                def mark(i, u, b, k):
                    dve.wait_ge(dst_in[u], i * 16 + 16)
                    nc.vector.tensor_scalar(onehot[:, k], dstb[:, u, :].rearrange("p (n j) -> p j n", j=J), node[:, bass.ds(b, 1)], None, ALU.is_equal).then_inc(onehot_done, 1)

                def edge_scores(i, u, s, k):
                    dve.wait_ge(ew_in[u], i * 16 + 16)
                    nc.vector.tensor_scalar(ew_term[:, k, :], ew[:, u, :], wb[:, 0:1], wb[:, 1:2], ALU.mult, ALU.add).then_inc(ew_done, 1)
                    dve.wait_ge(rows_in[u], i * (16 * J) + 16 * J)
                    dve.wait_ge(q_edges, s + 1)
                    dve.wait_ge(ew_done, s + 1)
                    for j in range(J):
                        last = nc.vector.tensor_tensor_reduce(out=product[:, j, 0:D1], in0=banks[j][:, 0:D1], in1=rows[:, u, j, :], scale=SCALE,
                                                              scalar=ew_term[:, k, j:j + 1], op0=ALU.mult, op1=ALU.add, accum_out=score[:, k, j:j + 1])
                    last.then_inc(scored, 1)

                def add_sums(s, k, b):
                    dve.wait_ge(summed, s + (1 + U))
                    dve.wait_ge(added, s + 1)
                    a = acc[:, bass.ds(b, 1), :]
                    nc.vector.scalar_tensor_tensor(out=a, in0=a, scalar=decay[:, k:k + 1], in1=banks[6 + k][:, 0:D1], op0=ALU.mult, op1=ALU.add).then_inc(added, 1)

                first = [dve.alloc_register(f"first{u}") for u in range(2)]
                for u in range(2):
                    dve.load([first[u]], step_block[u][0:1, FIRST:FIRST + 1])
                b0, b1_ = (dve.snap(r, min_val=0, max_val=B) for r in first)
                dve.sem_inc(added, 1)
                dve.sem_inc(max_kept, 1)
                mark(0, 0, b0, 0)
                mark(0, 1, b1_, 1)
                dve.wait_ge(ones_set, 1)
                edge_scores(0, 0, 0, 0)
                prev = dve.alloc_register("previous_block")
                with dve.Fori(0, n) as i:
                    blocks = listed(dve, regs, step_block[0], i)
                    nexts = listed(dve, ahead, step_block[2], i)
                    for u in range(U):
                        s, k, b = i * U + u, u % 2, blocks[u]
                        dve.wait_ge(max_kept, s + 1)
                        nc.vector.tensor_scalar(old_max, neg_max[:, bass.ds(b, 1)], 0.0, None, ALU.add).then_inc(max_read, 1)
                        dve.wait_ge(ones_set, 1)
                        dve.wait_ge(spread, s + 1)
                        dve.wait_ge(outside_done, s + 1)
                        dve.wait_ge(max_read, s + 1)
                        nc.vector.tensor_tensor_reduce(out=masked, in0=banks[4][:], in1=outside[:, k, :], scale=-1.0, scalar=old_max,
                                                       op0=ALU.add, op1=ALU.min, accum_out=new_max).then_inc(masked_done, 1)
                        dve.wait_ge(masked_done, s + 1)
                        nc.vector.tensor_tensor(max_step, new_max, old_max, ALU.subtract).then_inc(max_done, 1)
                        nc.vector.tensor_scalar(neg_max[:, bass.ds(b, 1)], new_max, 0.0, None, ALU.add).then_inc(max_kept, 1)
                        if u + 2 < U:
                            mark(i, u + 2, nexts[u], k)
                        else:
                            mark(i + 1, u + 2 - U, nexts[u], k)
                        edge_scores(i if u + 1 < U else i + 1, (u + 1) % U, s + 1, 1 - k)
                        add_sums(s, k, b)

        used[0] = 0
        inv_sum = part(NB)
        weight_sum = part(NB)
        floor_sum = part(NB)
        u_rows = part(2 * D).rearrange("p (k n) -> p k n", k=2)
        u_T = part(2 * D).rearrange("p (k n) -> p k n", k=2)
        r_in = part(2 * D).rearrange("p (k n) -> p k n", k=2)
        y_mid = part(2 * D).rearrange("p (k n) -> p k n", k=2)
        y_rows = part(2 * D).rearrange("p (k n) -> p k n", k=2)
        y_scaled = part(2 * D).rearrange("p (k n) -> p k n", k=2)
        fT = part(2 * F).rearrange("p (k n) -> p k n", k=2)
        x_again = part(2 * D).rearrange("p (k n) -> p k n", k=2)
        o_rows = part(2 * D).rearrange("p (k n) -> p k n", k=2)

        inv_link, inv_done = sem("inv_link"), sem("inv_done")
        r_back = [sem(f"r_back{k}") for k in range(2)]
        u_done, uT_ready, uT_copied, o_ready, y_half, y_done = (sem(n) for n in ("u_done", "uT_ready", "uT_copied", "o_ready", "y_half", "y_done"))
        n_done, g_half, y_ready, yT_ready, yT_copied, ff1_ready, gelu_done, ff2_ready, z_half, z_done = (
            sem(n) for n in ("n_done", "g_half", "y_ready", "yT_ready", "yT_copied", "ff1_ready", "gelu_done", "ff2_ready", "z_half", "z_done"))
        x_back = [sem(f"x_back{k}") for k in range(2)]
        zn_done, zg_done, zb_done, o_done = (sem(n) for n in ("zn_done", "zg_done", "zb_done", "o_done"))
        o_stored = [sem(f"o_stored{k}") for k in range(2)]
        PAIRS = NB // 2

        with nc.Block() as block:
            @block.sync
            def _(sp):
                for k in range(2):
                    sp.dma_start(r_in[:, k, :], r_rows[k * P:(k + 1) * P, :]).then_inc(r_back[k], 16)
                with sp.Fori(1, PAIRS) as i:
                    for k in range(2):
                        sp.wait_ge(y_half, i * 2 + (k - 1))
                        sp.dma_start(r_in[:, k, :], r_rows[bass.ds((i * 2 + k) * P, P), :]).then_inc(r_back[k], 16)
                for k in range(2):
                    sp.dma_start(x_again[:, k, :], x[k * P:(k + 1) * P, :]).then_inc(x_back[k], 16)
                for k in range(2):
                    sp.wait_ge(o_done, k + 1)
                    sp.dma_start(out[k * P:(k + 1) * P, :], o_rows[:, k, :]).then_inc(o_stored[k], 16)
                    sp.dma_start(x_again[:, k, :], x[(2 + k) * P:(3 + k) * P, :]).then_inc(x_back[k], 16)
                with sp.Fori(1, FULL // 2 - 1) as i:
                    for k in range(2):
                        sp.wait_ge(o_done, i * 2 + (k + 1))
                        sp.dma_start(out[bass.ds((i * 2 + k) * P, P), :], o_rows[:, k, :]).then_inc(o_stored[k], 16)
                        sp.dma_start(x_again[:, k, :], x[bass.ds((i * 2 + k + 2) * P, P), :]).then_inc(x_back[k], 16)
                for k in range(2):
                    b = FULL - 2 + k
                    sp.wait_ge(o_done, b + 1)
                    sp.dma_start(out[b * P:(b + 1) * P, :], o_rows[:, k, :]).then_inc(o_stored[k], 16)
                    if k == 0:
                        sp.dma_start(x_again[0:REST, 0, :], x[FULL * P:N, :]).then_inc(x_back[0], 16)
                sp.wait_ge(o_done, FULL + 1)
                sp.dma_start(out[FULL * P:N, :], o_rows[0:REST, 0, :]).then_inc(o_stored[0], 16)
                sp.wait_ge(o_stored[0], 16 * (FULL // 2 + 1))
                sp.wait_ge(o_stored[1], 16 * (FULL // 2))

            @block.scalar
            def _(act):
                act.wait_ge(inv_done, 1)

                def scale_u(i, k):
                    nc.scalar.activation(u_rows[:, k, :], acc[:, bass.ds(i, 1), 0:D], ACT.Copy, scale=inv_sum[:, bass.ds(i, 1)]).then_inc(u_done, 1)

                scale_u(0, 0)
                scale_u(1, 1)
                with act.Fori(1, PAIRS) as i:
                    for k in range(2):
                        act.wait_ge(uT_ready, i * 2 + (k - 1))
                        act.wait_ge(inv_done, 1)
                        scale_u(i * 2 + k, k)
                act.wait_ge(var_done, 2)
                nc.scalar.activation(tmp[:], rstd[:], ACT.Sqrt, bias=eps[:, 0:1]).then_inc(std_done, 1)
                act.wait_ge(ln_done, 2)

                def normalise(i, k, sem_done):
                    nc.scalar.activation(u_rows[:, k, :], acc[:, bass.ds(i, 1), 0:D], ACT.Identity, bias=nmr[:, bass.ds(i, 1)], scale=rstd[:, bass.ds(i, 1)]).then_inc(sem_done, 1)

                def gelu(i, k):
                    act.wait_ge(ff1_ready, i + 1)
                    for c in range(FC):
                        last = nc.scalar.activation(fT[:, k, c * P:(c + 1) * P], banks[2 + k][:, c * P:(c + 1) * P], ACT.Gelu_apprx_tanh, bias=bff1_col[:, c:c + 1])
                    last.then_inc(gelu_done, 1)

                normalise(0, 0, n_done)
                normalise(1, 1, n_done)
                with act.Fori(1, PAIRS) as i:
                    for k in range(2):
                        gelu(i * 2 + (k - 2), k)
                        act.wait_ge(g_half, i * 2 + (k - 1))
                        act.wait_ge(inv_done, 1)
                        normalise(i * 2 + k, k, n_done)
                for k in range(2):
                    gelu(NB - 2 + k, k)
                act.wait_ge(var_done, 3)
                nc.scalar.activation(tmp[:], rstd[:], ACT.Sqrt, bias=eps[:, 0:1]).then_inc(std_done, 1)
                act.wait_ge(ln_done, 3)
                normalise(0, 0, zn_done)
                normalise(1, 1, zn_done)
                with act.Fori(1, FULL // 2) as i:
                    for k in range(2):
                        act.wait_ge(zg_done, i * 2 + (k - 1))
                        act.wait_ge(inv_done, 1)
                        normalise(i * 2 + k, k, zn_done)
                act.wait_ge(zg_done, FULL - 1)
                normalise(FULL, 0, zn_done)

            @block.gpsimd
            def _(pool):
                def scale_y(i, k):
                    pool.wait_ge(n_done, i + 1)
                    nc.gpsimd.tensor_tensor(y_scaled[:, k, :], u_rows[:, k, :], row_of["g1"], ALU.mult).then_inc(g_half, 1)
                    pool.wait_ge(g_half, i + 1)
                    nc.gpsimd.tensor_tensor(y_rows[:, k, :], y_scaled[:, k, :], row_of["b1"], ALU.add).then_inc(y_ready, 1)

                scale_y(0, 0)
                scale_y(1, 1)
                with pool.Fori(1, PAIRS) as i:
                    for k in range(2):
                        pool.wait_ge(z_half, i * 2 + (k - 1))
                        scale_y(i * 2 + k, k)

                def scale_z(i, k):
                    pool.wait_ge(zn_done, i + 1)
                    nc.gpsimd.tensor_tensor(y_scaled[:, k, :], u_rows[:, k, :], row_of["g2"], ALU.mult).then_inc(zg_done, 1)

                scale_z(0, 0)
                scale_z(1, 1)
                with pool.Fori(1, FULL // 2) as i:
                    for k in range(2):
                        pool.wait_ge(zb_done, i * 2 + (k - 1))
                        scale_z(i * 2 + k, k)
                pool.wait_ge(zb_done, FULL - 1)
                scale_z(FULL, 0)

            @block.vector
            def _(dve):
                nc.vector.tensor_scalar(floor_sum, acc[:, :, D], 1e-12, None, ALU.max).then_inc(inv_link, 1)
                dve.wait_ge(inv_link, 1)
                nc.vector.reciprocal(inv_sum, floor_sum).then_inc(inv_link, 1)
                dve.wait_ge(inv_link, 2)
                nc.vector.tensor_tensor(weight_sum, acc[:, :, D], inv_sum, ALU.mult).then_inc(inv_done, 1)
                dve.wait_ge(inv_done, 1)

                def copy_uT(i, k):
                    dve.wait_ge(uT_ready, i + 1)
                    nc.vector.tensor_copy(u_T[:, k, :], banks[k][:, 0:D]).then_inc(uT_copied, 1)

                def first_sum(i, k, n, more):
                    if more:
                        copy_uT(i + 1, 1 - k)
                    dve.wait_ge(r_back[k], n * 16 + 16)
                    nc.vector.scalar_tensor_tensor(out=y_mid[:, k, :], in0=row_of["bv"], scalar=weight_sum[:, bass.ds(i, 1)], in1=r_in[:, k, :],
                                                   op0=ALU.mult, op1=ALU.add).then_inc(y_half, 1)
                    dve.wait_ge(o_ready, i + 1)
                    dve.wait_ge(y_half, i + 1)
                    nc.vector.tensor_tensor(acc[:, bass.ds(i, 1), 0:D], y_mid[:, k, :], banks[2 + k][:, 0:D], ALU.add).then_inc(y_done, 1)
                    dve.wait_ge(y_done, i + 1)
                    dve.wait_ge(inv_done, 1)
                    return nc.vector.bn_stats(stats[:, bass.ds(i, 1), :], acc[:, bass.ds(i, 1), 0:D])

                copy_uT(0, 0)
                with dve.Fori(0, PAIRS - 1) as i:
                    for k in range(2):
                        first_sum(i * 2 + k, k, i, True)
                first_sum(NB - 2, 0, PAIRS - 1, True)
                first_sum(NB - 1, 1, PAIRS - 1, False).then_inc(stats_done, 1)
                layer_stats(dve, 1)

                def copy_yT(i, k):
                    dve.wait_ge(yT_ready, i + 1)
                    nc.vector.tensor_copy(u_T[:, k, :], banks[k][:, 0:D]).then_inc(yT_copied, 1)

                def second_sum(i, k, more):
                    if more:
                        copy_yT(i + 1, 1 - k)
                    dve.wait_ge(ff2_ready, i + 1)
                    nc.vector.tensor_tensor(y_mid[:, k, :], banks[4 + k][:, 0:D], y_rows[:, k, :], ALU.add).then_inc(z_half, 1)
                    dve.wait_ge(z_half, i + 1)
                    nc.vector.tensor_tensor(acc[:, bass.ds(i, 1), 0:D], y_mid[:, k, :], row_of["b_ff2"], ALU.add).then_inc(z_done, 1)
                    dve.wait_ge(z_done, i + 1)
                    dve.wait_ge(inv_done, 1)
                    return nc.vector.bn_stats(stats[:, bass.ds(i, 1), :], acc[:, bass.ds(i, 1), 0:D])

                copy_yT(0, 0)
                with dve.Fori(0, PAIRS - 1) as i:
                    for k in range(2):
                        second_sum(i * 2 + k, k, True)
                second_sum(NB - 2, 0, True)
                second_sum(NB - 1, 1, False).then_inc(stats_done, 1)
                layer_stats(dve, 2)

                def third_sum(i, k, n, rows):
                    dve.wait_ge(zg_done, i + 1)
                    nc.vector.tensor_tensor(y_mid[:, k, :], y_scaled[:, k, :], row_of["b2"], ALU.add).then_inc(zb_done, 1)
                    dve.wait_ge(x_back[k], n * 16 + 16)
                    dve.wait_ge(zb_done, i + 1)
                    nc.vector.tensor_tensor(o_rows[0:rows, k, :], y_mid[0:rows, k, :], x_again[0:rows, k, :], ALU.add).then_inc(o_done, 1)

                third_sum(0, 0, 0, P)
                third_sum(1, 1, 0, P)
                with dve.Fori(1, FULL // 2) as i:
                    for k in range(2):
                        dve.wait_ge(o_stored[k], i * 16)
                        third_sum(i * 2 + k, k, i, P)
                dve.wait_ge(o_stored[0], (FULL // 2) * 16)
                third_sum(FULL, 0, FULL // 2, REST)

            @block.tensor
            def _(pe):
                def transpose_u(i, k):
                    pe.wait_ge(u_done, i + 1)
                    for c in range(DC):
                        last = nc.tensor.transpose(banks[k][:, c * P:(c + 1) * P], u_rows[:, k, c * P:(c + 1) * P], ident[:])
                    last.then_inc(uT_ready, 1)

                def output(i, k, more):
                    if more:
                        transpose_u(i + 1, 1 - k)
                    pe.wait_ge(uT_copied, i + 1)
                    for c in range(DC):
                        last = nc.tensor.matmul(banks[2 + k][:, 0:D], u_T[:, k, c * P:(c + 1) * P], wv_sb[:, c, :], start=(c == 0), stop=(c == DC - 1))
                    last.then_inc(o_ready, 1)

                transpose_u(0, 0)
                output(0, 0, True)
                output(1, 1, True)
                with pe.Fori(1, PAIRS - 1) as i:
                    for k in range(2):
                        pe.wait_ge(y_done, i * 2 + (k - 1))
                        output(i * 2 + k, k, True)
                for k in range(2):
                    pe.wait_ge(y_done, NB - 3 + k)
                    output(NB - 2 + k, k, k == 0)

                def transpose_y(i, k):
                    pe.wait_ge(y_ready, i + 1)
                    for c in range(DC):
                        last = nc.tensor.transpose(banks[k][:, c * P:(c + 1) * P], y_rows[:, k, c * P:(c + 1) * P], ident[:])
                    last.then_inc(yT_ready, 1)

                def feed_forward(i, k):
                    pe.wait_ge(yT_copied, i + 1)
                    for m in range(FC):
                        for c in range(DC):
                            last = nc.tensor.matmul(banks[2 + k][:, m * P:(m + 1) * P], w1_sb[:, c, m * P:(m + 1) * P], u_T[:, k, c * P:(c + 1) * P], start=(c == 0), stop=(c == DC - 1))
                    last.then_inc(ff1_ready, 1)

                def contract(i, k):
                    pe.wait_ge(gelu_done, i + 1)
                    for m in range(FC):
                        last = nc.tensor.matmul(banks[4 + k][:, 0:D], fT[:, k, m * P:(m + 1) * P], w2_sb[:, m, :], start=(m == 0), stop=(m == FC - 1))
                    last.then_inc(ff2_ready, 1)

                transpose_y(0, 0)
                feed_forward(0, 0)
                transpose_y(1, 1)
                feed_forward(1, 1)
                contract(0, 0)
                transpose_y(2, 0)
                with pe.Fori(1, PAIRS - 1) as i:
                    for k in range(2):
                        feed_forward(i * 2 + k, k)
                        contract(i * 2 + (k - 1), 1 - k)
                        transpose_y(i * 2 + (k + 1), 1 - k)
                feed_forward(NB - 2, 0)
                contract(NB - 3, 1)
                transpose_y(NB - 1, 1)
                feed_forward(NB - 1, 1)
                contract(NB - 2, 0)
                contract(NB - 1, 1)


_INS = ["x", "src", "dst", "edge_weight"] + ["L0_gnn_" + n for n in (
    "wq", "bq", "wk", "bk", "wv", "bv", "ws", "bs", "we", "be", "g1", "b1", "g2", "b2", "w_ff1", "b_ff1", "w_ff2", "b_ff2")]


def build(nc, shapes):
    args = [nc.dram_tensor(f"in_{n}", s, d, kind="ExternalInput").ap() for n, s, d in shapes]
    out = nc.dram_tensor("out", shapes[0][1], F32, kind="ExternalOutput").ap()
    gnn_layer(nc, *args, out)


def kernel(**inputs):
    import numpy as np
    import concourse.bacc as bacc
    from concourse.bass_utils import run_bass_kernel_spmd

    nc = bacc.Bacc("TRN2", target_bir_lowering=False, num_devices=1)
    arrays = {n: np.ascontiguousarray(inputs[n]) for n in _INS}
    build(nc, [(n, arrays[n].shape, mybir.dt.from_np(arrays[n].dtype)) for n in _INS])
    r = run_bass_kernel_spmd(nc, [{f"in_{n}": a for n, a in arrays.items()}], core_ids=[0])
    return r.results[0]["out"]
```

```python
from contextlib import ExitStack

import concourse.bass as bass
from concourse import mybir

F32 = mybir.dt.float32
BF16 = mybir.dt.bfloat16
I32 = mybir.dt.int32
ALU = mybir.AluOpType
ACT = mybir.ActivationFunctionType
AX_X = mybir.AxisListType.X

P = 128
J = 4
C = P * J
U = 8
S = 4
WINDOW = 16
BIG = 1e30
NO_MAX = 5e29
PAD_DST = 32767
FIRST = 16 - S
EPS = 1e-5


def ceil_div(a, b):
    return -(-a // b)


def gnn_layer(nc, x, src, dst, edge_weight, wq, bq, wk, bk, wv, bv, ws, bs, we, be, g1, b1, g2, b2,
              w_ff1, b_ff1, w_ff2, b_ff2, out):
    N, D = x.shape
    E = src.shape[0]
    F = w_ff1.shape[1]
    DC, FC = D // P, F // P
    D1 = D + 1
    SCALE = float(D) ** -0.5
    FULL = N // P
    REST = N - FULL * P
    B = ceil_div(N, P)
    NB = B + 1
    T = ceil_div(E, C)
    EP = T * C
    assert D == 2 * P and NB % 2 == 0 and REST > 0 and FULL % 2 == 0 and E % 16 == 0
    PAD = EP - E + 16
    ALL_STEPS = ceil_div(T * B, U) * U
    STAIR_STEPS = ceil_div(T + B - 1, U) * U
    HEAD = min(STAIR_STEPS + 8, T * B)
    TAIL = ALL_STEPS + WINDOW - T * B
    LEN = FIRST + ALL_STEPS + WINDOW
    TRIPS, STAIR_TRIPS = ALL_STEPS // U, STAIR_STEPS // U
    TG = ceil_div(T, P)
    assert HEAD <= min(2 * T, 512)

    ctx = ExitStack()
    with ctx:
        def sb(name, shape, dt=F32):
            return ctx.enter_context(nc.sbuf_tensor(name, shape, dt))

        def sem(name):
            return ctx.enter_context(nc.semaphore(name))

        def dram(name, shape, dt=F32):
            return nc.dram_tensor(name, shape, dt).ap()

        h_rows = dram("h_rows", (NB * P, D))
        r_rows = dram("r_rows", (NB * P, D))
        src_pad = dram("src_pad", (1, EP + 16), I32)
        dst_pad = dram("dst_pad", (1, EP + 16), I32)
        ew_pad = dram("ew_pad", (1, EP + 16))
        step_chunk = dram("step_chunk", (1, LEN), I32)
        step_block = dram("step_block", (1, LEN), I32)
        windows = dram("windows", (TRIPS + 1, WINDOW), I32)

        acc = sb("acc", [P, NB, D1])
        q3 = sb("q3", [P, NB, 3, D1 + 1], BF16)
        ident = sb("ident", [P, P])
        ones = sb("ones", [P, P])
        onesb = sb("onesb", [P, 1], BF16)
        wv_sb = sb("wv_sb", [P, DC, D])
        w1_sb = sb("w1_sb", [P, DC, F])
        w2_sb = sb("w2_sb", [P, FC, D])
        bias_names = ["bs", "bv", "g1", "b1", "g2", "b2", "b_ff2"]
        bias = sb("bias", [P, len(bias_names), D])
        row_of = {n: bias[:, k, :] for k, n in enumerate(bias_names)}
        bff1_col = sb("bff1_col", [P, FC])
        wb = sb("wb", [P, 2])
        stats = sb("stats", [P, NB, 6])
        mean = sb("mean", [P, NB])
        rstd = sb("rstd", [P, NB])
        nmr = sb("nmr", [P, NB])
        tmp = sb("tmp", [P, NB])
        eps = sb("eps", [P, 1])
        node = sb("node", [P, NB])
        neg_max = sb("neg_max", [P, NB])
        n_trips = sb("n_trips", [1, 1], I32)
        idx = sb("idx", [P, S, J], I32)
        ew = sb("ew", [P, S, J])
        dstb = sb("dstb", [P, S, C], I32)
        onehot = sb("onehot", [P, 2, J, P], BF16)
        WORK = 8420
        work = sb("work", [P, WORK])

        used = [0]

        def part(n, dt=F32):
            used[0] += n
            assert used[0] <= WORK, used
            a = work[:, used[0] - n:used[0]]
            return a if dt == F32 else a.bitcast(dt)

        banks = [ctx.enter_context(nc.psum_tensor(f"bank{k}", [P, 512], F32)) for k in range(8)]

        used[0] = 0
        wq_sb = part(DC * D).rearrange("p (c n) -> p c n", c=DC)
        wk_sb = part(DC * D).rearrange("p (c n) -> p c n", c=DC)
        ws_sb = part(DC * D).rearrange("p (c n) -> p c n", c=DC)
        wqT = part(DC * D).rearrange("p (c n) -> p c n", c=DC)
        wkT = part(DC * D1).rearrange("p (c n) -> p c n", c=DC)
        wqk = part(DC * D1).rearrange("p (c n) -> p c n", c=DC)
        bq_col = part(DC)
        q_bias = part(D1)
        h_now = part(2 * D).rearrange("p (k n) -> p k n", k=2)
        hT = part(2 * D).rearrange("p (k n) -> p k n", k=2)
        qf = part(D1)
        q_rest = part(D1)
        r_mid = part(D)
        r_out = part(2 * D).rearrange("p (k n) -> p k n", k=2)
        srow = part(HEAD)
        stair_t, stair_b, all_t, all_b = (part(HEAD) for _ in range(4))
        spare = dstb[:].rearrange("p u n -> p (u n)")
        row_t, row_b = spare[:, 0:HEAD], spare[:, HEAD:2 * HEAD]
        before = spare[:, 2 * HEAD:2 * HEAD + TG * HEAD // 2].bitcast(BF16).rearrange("p (g s) -> p g s", g=TG)
        ends_i = part(TG, I32)
        chunk_i = part(TG, I32)
        chunk_f = part(TG)
        ends = part(TG)
        falls = part(1)
        is_sorted = part(1)
        trips_f = part(1)
        node_i = part(NB, I32)
        padding = part(PAD, I32)
        zeros_i = part(PAD, I32)
        tail_t = part(TAIL, I32)
        tail_b = part(TAIL, I32)
        q3f = q3[:].rearrange("p b k n -> p (b k n)")
        EDGES_P = EP // P
        early = sb("early", [P, 2 * EDGES_P], I32)
        dst_a, dst_b = early[:, 0:EDGES_P], early[:, EDGES_P:2 * EDGES_P]
        pair_t = sb("pair_t", [B, T], I32)
        pair_b = sb("pair_b", [B, T], I32)

        ident_set, consts = sem("ident_set"), sem("consts")
        x_in = [sem(f"x_in{k}") for k in range(4)]
        x_rest_in, x_zero = sem("x_rest_in"), sem("x_zero")
        w_in, late_in = sem("w_in"), sem("late_in")
        edges_in, check_in, ends_in = sem("edges_in"), sem("check_in"), sem("ends_in")
        wT_ready, wT_copied, wqk_ready, wqk_copied = sem("wT_ready"), sem("wT_copied"), sem("wqk_ready"), sem("wqk_copied")
        stats_done, ln_link, var_done, std_done, ln_done = (sem(n) for n in ("stats_done", "ln_link", "var_done", "std_done", "ln_done"))
        h_done, h_stored, h_copied = sem("h_done"), sem("h_stored"), sem("h_copied")
        hT_ready, hT_copied = sem("hT_ready"), sem("hT_copied")
        q_ready, qf_done, hi_done, rest_done, mid_done, lo_done = (sem(n) for n in ("q_ready", "qf_done", "hi_done", "rest_done", "mid_done", "lo_done"))
        hws_ready, r_half, r_done = sem("hws_ready"), sem("r_half"), sem("r_done")
        r_stored = [sem(f"r_stored{k}") for k in range(2)]
        pairs_set, pairs_out = sem("pairs_set"), sem("pairs_out")
        windows_out = sem("windows_out")
        plan, counts_ready, plan_done, heads_out = sem("plan"), sem("counts_ready"), sem("plan_done"), sem("heads_out")
        cleared = sem("cleared")

        def columns(v, n):
            return v.rearrange("(c p) -> p c", p=P)

        def every(v):
            return v.rearrange("(a n) -> a n", a=1).to_broadcast((P, v.shape[0]))

        def step_windows(first, end):
            return bass.AP(tensor=step_block.tensor, offset=FIRST - 1 + first * U, ap=[[U, end - first], [1, WINDOW]])

        def layer_stats(dve, turn):
            n = [5 * turn + 1]

            def link(i):
                i.then_inc(ln_link, 1)
                n[0] += 1
                dve.wait_ge(ln_link, n[0])

            dve.wait_ge(stats_done, turn + 1)
            nc.vector.tensor_tensor(mean[:], stats[:, :, 1], stats[:, :, 4], ALU.add)
            link(nc.vector.tensor_tensor(tmp[:], stats[:, :, 1], stats[:, :, 4], ALU.subtract))
            nc.vector.tensor_tensor(rstd[:], stats[:, :, 2], stats[:, :, 5], ALU.add)
            link(nc.vector.tensor_tensor(tmp[:], tmp[:], tmp[:], ALU.mult))
            nc.vector.tensor_scalar(mean[:], mean[:], 0.5, None, ALU.mult)
            link(nc.vector.tensor_scalar(tmp[:], tmp[:], 0.25, None, ALU.mult))
            nc.vector.scalar_tensor_tensor(out=rstd[:], in0=rstd[:], scalar=1.0 / D, in1=tmp[:], op0=ALU.mult, op1=ALU.add).then_inc(var_done, 1)
            dve.wait_ge(std_done, turn + 1)
            link(nc.vector.reciprocal(rstd[:], tmp[:]))
            link(nc.vector.scalar_tensor_tensor(out=nmr[:], in0=mean[:], scalar=-1.0, in1=rstd[:], op0=ALU.mult, op1=ALU.mult))
            nc.vector.tensor_copy(tmp[:], nmr[:]).then_inc(ln_done, 1)

        XG = FULL // 4
        with nc.Block() as block:
            @block.sync
            def _(sp):
                for k in range(4):
                    sp.dma_start(acc[:, k * XG:(k + 1) * XG, 0:D],
                                 x[k * XG * P:(k + 1) * XG * P, :].rearrange("(b p) d -> p b d", p=P)).then_inc(x_in[k], 16)
                sp.wait_ge(x_zero, 1)
                sp.dma_start(acc[0:REST, FULL, 0:D], x[FULL * P:N, :]).then_inc(x_rest_in, 16)
                for a, b in ((src, src_pad), (dst, dst_pad), (edge_weight, ew_pad)):
                    sp.dma_start(b[0, 0:E].rearrange("(a n) -> a n", a=16), a.rearrange("(a n) -> a n", a=16)).then_inc(edges_in, 16)
                sp.wait_ge(consts, 1)
                for a, b in ((zeros_i, src_pad), (padding, dst_pad)):
                    sp.dma_start(b[0:1, E:E + PAD], a[0:1, :]).then_inc(edges_in, 16)
                sp.dma_start(ew_pad[0:1, E:E + PAD], zeros_i[0:1, :].bitcast(F32)).then_inc(edges_in, 16)
                sp.wait_ge(edges_in, 6 * 16)
                sp.dma_start(dst_a, dst_pad[0, 0:EP].rearrange("(p n) -> p n", p=P)).then_inc(check_in, 16)
                sp.dma_start(dst_b, dst_pad[0, 1:EP + 1].rearrange("(p n) -> p n", p=P)).then_inc(check_in, 16)
                sp.wait_ge(consts, 2)
                chunks = dst_pad[0, 0:EP].rearrange("(t c) -> t c", c=C)
                for g in range(TG):
                    n = min(P, T - g * P)
                    sp.dma_start(ends_i[0:n, g:g + 1], chunks[g * P:g * P + n, C - 1:C], allow_slow_non_contiguous=True).then_inc(ends_in, 16)
                sp.wait_ge(pairs_set, 1)
                for tab, pairs, tail in ((step_chunk, pair_t, tail_t), (step_block, pair_b, tail_b)):
                    sp.dma_start(tab[0, FIRST:FIRST + T * B].rearrange("(b t) -> b t", t=T), pairs[:, :]).then_inc(pairs_out, 16)
                    sp.dma_start(tab[0:1, FIRST + T * B:FIRST + T * B + TAIL], tail[0:1, :]).then_inc(pairs_out, 16)
                sp.dma_start(step_block[0:1, FIRST - 1:FIRST], tail_b[0:1, 0:1]).then_inc(pairs_out, 16)
                sp.wait_ge(pairs_out, 5 * 16)
                sp.dma_start(windows[STAIR_TRIPS + 1:TRIPS + 1, :], step_windows(STAIR_TRIPS + 1, TRIPS + 1)).then_inc(windows_out, 16)
                with sp.Fori(0, NB) as i:
                    sp.wait_ge(h_done, i + 1)
                    sp.dma_start(h_rows[bass.ds(i * P, P), :], acc[:, bass.ds(i, 1), 0:D]).then_inc(h_stored, 16)
                with sp.Fori(0, NB // 2) as i:
                    for k in range(2):
                        sp.wait_ge(r_done, i * 2 + (k + 1))
                        sp.dma_start(r_rows[bass.ds((i * 2 + k) * P, P), :], r_out[:, k, :]).then_inc(r_stored[k], 16)
                sp.wait_ge(plan_done, 1)
                sp.wait_ge(windows_out, 16)
                for tab, row in ((step_block, row_b), (step_chunk, row_t)):
                    sp.dma_start(tab[0:1, FIRST:FIRST + HEAD], row[0:1, :]).then_inc(heads_out, 16)
                sp.wait_ge(heads_out, 2 * 16)
                sp.dma_start(windows[0:STAIR_TRIPS + 1, :], step_windows(0, STAIR_TRIPS + 1)).then_inc(windows_out, 16)
                for k in range(2):
                    sp.wait_ge(r_stored[k], 16 * (NB // 2))
                sp.wait_ge(h_stored, 16 * NB)
                sp.wait_ge(windows_out, 2 * 16)
                sp.wait_ge(late_in, 16 * 12)

            @block.gpsimd
            def _(pool):
                pool.memset(ident[:], 0.0).then_inc(ident_set, 1)
                pool.wait_ge(ident_set, 1)
                pool.affine_select(out=ident[:], in_=ident[:], compare_op=ALU.not_equal, fill=1.0, base=0,
                                   pattern=[[-1, P]], channel_multiplier=1).then_inc(ident_set, 1)
                pool.memset(zeros_i[0:1, :], 0)
                pool.memset(padding[0:1, :], PAD_DST).then_inc(consts, 1)
                pool.memset(ends_i, PAD_DST).then_inc(consts, 1)
                pool.memset(tail_t[0:1, :], 0)
                pool.memset(tail_b[0:1, :], B)
                pool.iota(pair_t[:, :], [[1, T]], base=0, channel_multiplier=0)
                pool.iota(pair_b[:, :], [[0, T]], base=0, channel_multiplier=1).then_inc(pairs_set, 1)
                pool.iota(row_t, [[1, HEAD]], base=0, channel_multiplier=0)
                pool.iota(chunk_i, [[P, TG]], base=0, channel_multiplier=1)
                pool.iota(node_i, [[P, NB]], base=0, channel_multiplier=1).then_inc(consts, 1)

                def copy_h(i, k):
                    pool.wait_ge(h_done, i + 1)
                    pool.wait_ge(ident_set, 2)
                    nc.gpsimd.tensor_copy(h_now[:, k, :], acc[:, bass.ds(i, 1), 0:D]).then_inc(h_copied, 1)

                copy_h(0, 0)
                copy_h(1, 1)
                with pool.Fori(1, NB // 2) as i:
                    for k in range(2):
                        pool.wait_ge(hT_ready, i * 2 + (k - 1))
                        copy_h(i * 2 + k, k)

            @block.scalar
            def _(act):
                for w, t in ((wq, wq_sb), (wk, wk_sb), (ws, ws_sb)):
                    act.dma_start(t, w.rearrange("(c p) n -> p c n", p=P)).then_inc(w_in, 16)
                with nc.allow_non_contiguous_dma("columns of two biases"):
                    act.dma_start(wkT[:, :, D], columns(bk, DC)).then_inc(w_in, 16)
                    act.dma_start(bq_col, columns(bq, DC)).then_inc(w_in, 16)
                    act.dma_start(bff1_col[:], columns(b_ff1, FC)).then_inc(late_in, 16)
                for n, v in zip(bias_names, (bs, bv, g1, b1, g2, b2, b_ff2)):
                    act.dma_start(row_of[n], every(v)).then_inc(w_in if n == "bs" else late_in, 16)
                act.dma_start(wb[:, 0:1], every(we.rearrange("a b -> (a b)"))).then_inc(late_in, 16)
                act.dma_start(wb[:, 1:2], every(be)).then_inc(late_in, 16)
                act.dma_start(wv_sb[:], wv.rearrange("(c p) n -> p c n", p=P)).then_inc(late_in, 16)
                act.dma_start(w1_sb[:], w_ff1.rearrange("(c p) n -> p c n", p=P)).then_inc(late_in, 16)
                act.dma_start(w2_sb[:], w_ff2.rearrange("(c p) n -> p c n", p=P)).then_inc(late_in, 16)
                act.wait_ge(var_done, 1)
                nc.scalar.activation(tmp[:], rstd[:], ACT.Sqrt, bias=eps[:, 0:1]).then_inc(std_done, 1)
                act.wait_ge(ln_done, 1)
                with act.Fori(0, NB) as i:
                    a = acc[:, bass.ds(i, 1), 0:D]
                    nc.scalar.activation(a, a, ACT.Relu, bias=nmr[:, bass.ds(i, 1)], scale=rstd[:, bass.ds(i, 1)]).then_inc(h_done, 1)
                with act.Fori(0, NB) as i:
                    act.wait_ge(qf_done, i + 1)
                    act.wait_ge(ln_done, 1)
                    nc.scalar.copy(q3[:, bass.ds(i, 1), 0, 0:D1], qf).then_inc(hi_done, 1)
                    act.wait_ge(rest_done, i + 1)
                    act.wait_ge(ln_done, 1)
                    nc.scalar.copy(q3[:, bass.ds(i, 1), 1, 0:D1], q_rest).then_inc(mid_done, 1)

            @block.vector
            def _(dve):
                nc.vector.memset(acc[:, FULL:NB, :], 0.0).then_inc(x_zero, 1)
                nc.vector.memset(eps[:], EPS)
                nc.vector.memset(ones[:], 1.0)
                nc.vector.memset(onesb[:], 1.0)
                nc.vector.memset(neg_max[:], NO_MAX).then_inc(ln_link, 1)
                for k in range(2 * DC):
                    dve.wait_ge(wT_ready, k + 1)
                    nc.vector.tensor_copy((wqT if k < DC else wkT)[:, k % DC, 0:D], banks[k][:, 0:D]).then_inc(wT_copied, 1)
                for k in range(4):
                    dve.wait_ge(x_in[k], 16)
                    with dve.Fori(k * XG, (k + 1) * XG) as i:
                        nc.vector.bn_stats(stats[:, bass.ds(i, 1), :], acc[:, bass.ds(i, 1), 0:D])
                dve.wait_ge(x_rest_in, 16)
                for i in range(FULL, NB):
                    last = nc.vector.bn_stats(stats[:, i, :], acc[:, i, 0:D])
                last.then_inc(stats_done, 1)
                layer_stats(dve, 0)
                for k in range(DC):
                    dve.wait_ge(wqk_ready, k + 1)
                    nc.vector.tensor_copy(wqk[:, k, :], banks[4 + k][:, 0:D1]).then_inc(wqk_copied, 1)
                dve.wait_ge(wqk_ready, DC + 1)
                nc.vector.tensor_copy(q_bias, banks[6][:, 0:D1]).then_inc(wqk_copied, 1)
                dve.wait_ge(wqk_copied, DC + 1)
                dve.wait_ge(w_in, 6 * 16)

                def copy_hT(i, k):
                    dve.wait_ge(hT_ready, i + 1)
                    nc.vector.tensor_copy(hT[:, k, :], banks[0][:, 0:D]).then_inc(hT_copied, 1)

                def split_q(i, k, more):
                    if more:
                        copy_hT(i + 1, 1 - k)
                    dve.wait_ge(q_ready, i + 1)
                    nc.vector.tensor_tensor(qf, banks[1 + k][:, 0:D1], q_bias, ALU.add).then_inc(qf_done, 1)
                    dve.wait_ge(hi_done, i + 1)
                    nc.vector.tensor_tensor(q_rest, qf, q3[:, bass.ds(i, 1), 0, 0:D1], ALU.subtract).then_inc(rest_done, 1)
                    dve.wait_ge(hws_ready, i + 1)
                    nc.vector.tensor_tensor(r_mid, banks[3 + k][:, 0:D], row_of["bs"], ALU.add).then_inc(r_half, 1)
                    dve.wait_ge(r_half, i + 1)
                    nc.vector.tensor_tensor(r_out[:, k, :], r_mid, acc[:, bass.ds(i, 1), 0:D], ALU.add).then_inc(r_done, 1)
                    dve.wait_ge(mid_done, i + 1)
                    nc.vector.tensor_tensor(q3[:, bass.ds(i, 1), 2, 0:D1], q_rest, q3[:, bass.ds(i, 1), 1, 0:D1], ALU.subtract).then_inc(lo_done, 1)

                copy_hT(0, 0)
                split_q(0, 0, True)
                split_q(1, 1, True)
                with dve.Fori(1, NB // 2 - 1) as i:
                    for k in range(2):
                        dve.wait_ge(r_stored[k], i * 16)
                        split_q(i * 2 + k, k, True)
                for k in range(2):
                    dve.wait_ge(r_stored[k], (NB // 2 - 1) * 16)
                    split_q(NB - 2 + k, k, k == 0)
                dve.wait_ge(consts, 3)
                nc.vector.tensor_copy(srow, row_t)
                nc.vector.tensor_copy(node[:], node_i)
                nc.vector.tensor_copy(chunk_f, chunk_i)
                dve.wait_ge(ends_in, TG * 16)
                nc.vector.tensor_scalar(ends_i, ends_i, 7, None, ALU.arith_shift_right).then_inc(plan, 1)
                dve.wait_ge(plan, 1)
                nc.vector.scalar_tensor_tensor(out=ends, in0=ends_i, scalar=float(B - 1), in1=chunk_f, op0=ALU.min, op1=ALU.add).then_inc(plan, 1)
                dve.wait_ge(plan, 2)
                for g in range(TG):
                    nc.vector.tensor_scalar(before[:, g, :], srow, ends[:, g:g + 1], None, ALU.is_gt)
                dve.wait_ge(check_in, 32)
                nc.vector.tensor_tensor(dst_a, dst_a, dst_b, ALU.is_gt).then_inc(plan, 1)
                dve.wait_ge(plan, 3)
                nc.vector.tensor_reduce(falls, dst_a, AX_X, ALU.add).then_inc(plan, 1)
                dve.wait_ge(counts_ready, 1)
                cnt, bad = banks[7][0:1, 0:HEAD], banks[6][0:1, 0:1]
                nc.vector.tensor_scalar(is_sorted[0:1, :], bad, 0.0, None, ALU.is_equal)
                nc.vector.tensor_scalar(stair_t[0:1, :], cnt, float(T - 1), None, ALU.min)
                nc.vector.tensor_scalar(all_b[0:1, :], srow[0:1, :], float(T), None, ALU.is_ge).then_inc(plan, 1)
                dve.wait_ge(plan, 5)
                nc.vector.tensor_tensor(stair_b[0:1, :], srow[0:1, :], stair_t[0:1, :], ALU.subtract)
                nc.vector.scalar_tensor_tensor(out=all_t[0:1, :], in0=all_b[0:1, :], scalar=-float(T), in1=srow[0:1, :], op0=ALU.mult, op1=ALU.add)
                nc.vector.tensor_scalar(trips_f[0:1, :], is_sorted[0:1, :], float((STAIR_STEPS - ALL_STEPS) // U), float(ALL_STEPS // U), ALU.mult, ALU.add).then_inc(plan, 1)
                dve.wait_ge(plan, 6)
                nc.vector.tensor_copy(n_trips[:], trips_f[0:1, :])
                nc.vector.tensor_tensor(stair_t[0:1, :], stair_t[0:1, :], all_t[0:1, :], ALU.subtract)
                nc.vector.scalar_tensor_tensor(out=stair_b[0:1, :], in0=stair_b[0:1, :], scalar=float(B), in1=all_b[0:1, :], op0=ALU.min, op1=ALU.subtract).then_inc(plan, 1)
                dve.wait_ge(plan, 7)
                nc.vector.scalar_tensor_tensor(out=row_t[0:1, :], in0=stair_t[0:1, :], scalar=is_sorted[0:1, 0:1], in1=all_t[0:1, :], op0=ALU.mult, op1=ALU.add)
                nc.vector.scalar_tensor_tensor(out=row_b[0:1, :], in0=stair_b[0:1, :], scalar=is_sorted[0:1, 0:1], in1=all_b[0:1, :], op0=ALU.mult, op1=ALU.add).then_inc(plan_done, 1)
                dve.wait_ge(h_stored, 16 * NB)
                nc.vector.memset(acc[:], 0.0).then_inc(cleared, 1)

            @block.tensor
            def _(pe):
                pe.wait_ge(ident_set, 2)
                pe.wait_ge(w_in, 6 * 16)
                for k in range(2 * DC):
                    w = wq_sb if k < DC else wk_sb
                    c = k % DC
                    for r in range(DC):
                        last = nc.tensor.transpose(banks[k][:, r * P:(r + 1) * P], w[:, r, c * P:(c + 1) * P], ident[:])
                    last.then_inc(wT_ready, 1)
                pe.wait_ge(wT_copied, 2 * DC)
                for r in range(DC):
                    for c in range(DC):
                        last = nc.tensor.matmul(banks[4 + r][:, 0:D1], wqT[:, c, r * P:(r + 1) * P], wkT[:, c, :], start=(c == 0), stop=(c == DC - 1))
                    last.then_inc(wqk_ready, 1)
                for c in range(DC):
                    last = nc.tensor.matmul(banks[6][:, 0:D1], bq_col[:, c:c + 1].broadcast_to([P, P]), wkT[:, c, :], start=(c == 0), stop=(c == DC - 1))
                last.then_inc(wqk_ready, 1)

                def transpose_h(i, k):
                    pe.wait_ge(h_copied, i + 1)
                    for c in range(DC):
                        last = nc.tensor.transpose(banks[0][:, c * P:(c + 1) * P], h_now[:, k, c * P:(c + 1) * P], ident[:])
                    last.then_inc(hT_ready, 1)

                def project(i, k, more):
                    pe.wait_ge(hT_copied, i + 1)
                    if more:
                        transpose_h(i + 1, 1 - k)
                    for c in range(DC):
                        last = nc.tensor.matmul(banks[1 + k][:, 0:D1], hT[:, k, c * P:(c + 1) * P], wqk[:, c, :], start=(c == 0), stop=(c == DC - 1))
                    last.then_inc(q_ready, 1)
                    for c in range(DC):
                        last = nc.tensor.matmul(banks[3 + k][:, 0:D], hT[:, k, c * P:(c + 1) * P], ws_sb[:, c, :], start=(c == 0), stop=(c == DC - 1))
                    last.then_inc(hws_ready, 1)

                transpose_h(0, 0)
                pe.wait_ge(wqk_copied, DC + 1)
                with pe.Fori(0, NB // 2 - 1) as i:
                    for k in range(2):
                        project(i * 2 + k, k, True)
                project(NB - 2, 0, True)
                project(NB - 1, 1, False)
                pe.wait_ge(plan, 4)
                pe.wait_ge(r_done, NB)
                for g in range(TG):
                    nc.tensor.matmul(banks[7][0:1, 0:HEAD], onesb[:], before[:, g, :], start=(g == 0), stop=(g == TG - 1))
                nc.tensor.matmul(banks[6][0:1, 0:1], falls, ones[:, 0:1], start=True, stop=True).then_inc(counts_ready, 1)

        used[0] = 0
        rows = part(S * J * D1).rearrange("p (u j n) -> p u j n", u=S, j=J)
        masked = part(C)
        probsT = part(C)
        probs = part(C).rearrange("p (j n) -> p j n", j=J)
        outside = part(C, BF16)[:, 0:2 * C].rearrange("p (k n) -> p k n", k=2)
        product = part(J * (D1 + 1) // 2, BF16).rearrange("p (j n) -> p j n", j=J)
        score = part(2 * J).rearrange("p (k j) -> p k j", k=2)
        ew_term = part(2 * J).rearrange("p (k j) -> p k j", k=2)
        old_max = part(2)
        new_max = part(1)
        decay = part(2)

        ones_set, sums_set = sem("ones_set"), sem("sums_set")
        idx_in = [sem(f"idx_in{c}") for c in range(S)]
        ew_in = [sem(f"ew_in{c}") for c in range(S)]
        dst_in = [sem(f"dst_in{c}") for c in range(S)]
        rows_in = [sem(f"rows_in{c}") for c in range(S)]
        onehot_done, outside_done, q_edges, scored = sem("onehot_done"), sem("outside_done"), sem("q_edges"), sem("scored")
        ew_done, spread, max_read, masked_done, max_kept = (sem(n) for n in ("ew_done", "spread", "max_read", "masked_done", "max_kept"))
        exp_done, turned, probs_done, summed, added = (sem(n) for n in ("exp_done", "turned", "probs_done", "summed", "added"))

        def use(i, u):
            return i * (U // S) + u // S

        with nc.Block() as block:
            def trips(eng):
                return eng.value_load(n_trips[0:1, 0:1], min_val=STAIR_TRIPS, max_val=TRIPS)

            @block.sync
            def _(sp):
                n = trips(sp)
                regs = [sp.alloc_register(f"chunk{u}") for u in range(U)]

                def fetch(chunk, c):
                    at = chunk * C
                    sp.dma_start(idx[:, c, :], src_pad[0, bass.ds(at, C)].rearrange("(p j) -> p j", j=J)).then_inc(idx_in[c], 16)
                    sp.dma_start(dstb[:, c, :], dst_pad[0:1, bass.ds(at, C)].to_broadcast((P, C))).then_inc(dst_in[c], 16)
                    sp.dma_start(ew[:, c, :], ew_pad[0, bass.ds(at, C)].rearrange("(p j) -> p j", j=J)).then_inc(ew_in[c], 16)

                sp.load(regs[0:S], step_chunk[0:1, FIRST:FIRST + S])
                for c in range(S):
                    fetch(sp.snap(regs[c], min_val=0, max_val=T - 1), c)
                with sp.Fori(0, n) as i:
                    sp.load(regs, step_chunk[0:1, bass.ds(i * U + (FIRST + S), U)])
                    chunks = [sp.snap(r, min_val=0, max_val=T - 1) for r in regs]
                    for u in range(U):
                        gathered, used_steps = sp.to_reg(use(i, u) * (16 * J) + 16 * J), sp.to_reg(i * U + (u + 1))
                        sp.wait_ge(edges_in, 6 * 16)
                        sp.wait_ge(rows_in[u % S], gathered)
                        sp.wait_ge(onehot_done, used_steps)
                        sp.wait_ge(ew_done, used_steps)
                        fetch(chunks[u], u % S)
                landed = sp.to_reg(use(n, 0) * 16 + 16)
                sp.wait_ge(edges_in, 6 * 16)
                for c in range(S):
                    for landed_in in (idx_in[c], dst_in[c], ew_in[c]):
                        sp.wait_ge(landed_in, landed)

            @block.gpsimd
            def _(pool):
                n = trips(pool)

                def gather(i, u):
                    landed, free = pool.to_reg(use(i, u) * 16 + 16), pool.to_reg(i * U + (u + 1))
                    pool.wait_ge(h_stored, 16 * NB)
                    pool.wait_ge(summed, free)
                    pool.wait_ge(idx_in[u % S], landed)
                    for j in range(J):
                        pool.indirect_dma_start(rows[:, u % S, j, 0:D], None, h_rows, bass.IndirectOffsetOnAxis(idx[:, u % S, j:j + 1], 0)).then_inc(rows_in[u % S], 16)

                with pool.Fori(0, n) as i:
                    for u in range(U):
                        gather(i, u)
                gather(n, 0)
                pool.wait_ge(rows_in[0], use(n, 0) * (16 * J) + 16 * J)

            @block.tensor
            def _(pe):
                n = trips(pe)
                regs = [pe.alloc_register(f"next_block{u}") for u in range(U)]

                def expand_q(k, half, b):
                    for j in (2 * half, 2 * half + 1):
                        for c in range(3):
                            last = nc.tensor.matmul(banks[j][:, 0:D1], onehot[:, k, j, :], q3[:, bass.ds(b, 1), c, 0:D1], start=(c == 0), stop=(c == 2))
                    last.then_inc(q_edges, 1)

                def spread_scores(k):
                    for j in range(J):
                        last = nc.tensor.transpose(banks[4][:, j * P:(j + 1) * P], score[:, k, j:j + 1].broadcast_to([P, P]), ident[:])
                    last.then_inc(spread, 1)

                pe.load(regs[0:2], windows[0:1, 1:3])
                first = [pe.snap(r, min_val=0, max_val=B) for r in regs[0:2]]
                pe.sem_inc(summed, S)
                pe.wait_ge(onehot_done, 1)
                expand_q(0, 0, first[0])
                expand_q(0, 1, first[0])
                pe.wait_ge(onehot_done, 2)
                pe.wait_ge(scored, 1)
                expand_q(1, 0, first[1])
                pe.wait_ge(scored, 2)
                spread_scores(0)
                expand_q(1, 1, first[1])
                with pe.Fori(0, n) as i:
                    pe.load(regs, windows[bass.ds(i, 1), 3:3 + U])
                    blocks = [pe.snap(r, min_val=0, max_val=B) for r in regs]
                    for u in range(U):
                        s, k = i * U + u, u % 2
                        pe.wait_ge(exp_done, s + 1)
                        for half in (1, 0):
                            for j in range(2):
                                last = nc.tensor.transpose(banks[5 - half][:, j * P:(j + 1) * P], probsT[:, (2 * half + j) * P:(2 * half + j + 1) * P], ident[:])
                            last.then_inc(turned, 1)
                        pe.wait_ge(onehot_done, s + 3)
                        pe.wait_ge(scored, s * 2 + 3)
                        expand_q(k, 0, blocks[u])
                        pe.wait_ge(scored, s * 2 + 4)
                        pe.wait_ge(probs_done, s * 2 + 1)
                        spread_scores(1 - k)
                        expand_q(k, 1, blocks[u])
                        for j in (2, 3, 0, 1):
                            if j == 0:
                                pe.wait_ge(probs_done, s * 2 + 2)
                            last = nc.tensor.matmul(banks[6 + k][:, 0:D1], probs[:, j, :], rows[:, u % S, j, :], start=(j == 2), stop=(j == 1))
                        last.then_inc(summed, 1)

            @block.scalar
            def _(act):
                n = trips(act)

                def prepare(i, u, s, k):
                    act.wait_ge(onehot_done, s + 1)
                    nc.scalar.activation(outside[:, k, :], onehot[:, k].rearrange("p j n -> p (j n)"), ACT.Copy, scale=BIG, bias=-BIG).then_inc(outside_done, 1)
                    act.wait_ge(ew_in[u % S], use(i, u) * 16 + 16)
                    nc.scalar.activation(ew_term[:, k, :], ew[:, u % S, :], ACT.Identity, bias=wb[:, 1:2], scale=wb[:, 0:1]).then_inc(ew_done, 1)

                prepare(0, 0, 0, 0)
                prepare(0, 1, 1, 1)
                with act.Fori(0, n) as i:
                    for u in range(U):
                        s, k = i * U + u, u % 2
                        act.wait_ge(masked_done, s + 1)
                        nc.scalar.activation(decay[:, k:k + 1], old_max[:, k:k + 1], ACT.Exp, bias=new_max, scale=-1.0)
                        nc.scalar.activation(probsT, masked, ACT.Exp, bias=new_max, scale=-1.0).then_inc(exp_done, 1)
                        for half in (1, 0):
                            act.wait_ge(turned, s * 2 + (2 - half))
                            nc.scalar.copy(probs[:, 2 * half:2 * half + 2, :].rearrange("p j n -> p (j n)"), banks[5 - half][:, 0:2 * P]).then_inc(probs_done, 1)
                        prepare(i, u + 2, s + 2, k)

            @block.vector
            def _(dve):
                n = trips(dve)
                regs = [dve.alloc_register(f"block{u}") for u in range(U + 4)]
                nc.vector.memset(rows[:, :, :, D:D1], 1.0).then_inc(ones_set, 1)
                nc.vector.memset(banks[7][:, 0:D1], 0.0)
                nc.vector.memset(decay[:, 1:2], 1.0).then_inc(sums_set, 1)

                def mark(i, u, b):
                    dve.wait_ge(dst_in[u % S], use(i, u) * 16 + 16)
                    nc.vector.tensor_scalar(onehot[:, u % 2], dstb[:, u % S, :].rearrange("p (n j) -> p j n", j=J), node[:, bass.ds(b, 1)], None, ALU.is_equal).then_inc(onehot_done, 1)

                def edge_scores(i, u, s):
                    gathered, first_half, second_half = dve.to_reg(use(i, u) * (16 * J) + 16 * J), dve.to_reg(s * 2 + 1), dve.to_reg(s * 2 + 2)
                    dve.wait_ge(ones_set, 1)
                    dve.wait_ge(rows_in[u % S], gathered)
                    dve.wait_ge(ew_done, s + 1)
                    for half, ready in ((0, first_half), (1, second_half)):
                        dve.wait_ge(ones_set, 1)
                        dve.wait_ge(q_edges, ready)
                        for j in (2 * half, 2 * half + 1):
                            last = nc.vector.tensor_tensor_reduce(out=product[:, j, 0:D1], in0=banks[j][:, 0:D1], in1=rows[:, u % S, j, :], scale=SCALE,
                                                                  scalar=ew_term[:, u % 2, j:j + 1], op0=ALU.mult, op1=ALU.add, accum_out=score[:, u % 2, j:j + 1])
                        last.then_inc(scored, 1)

                def read_max(s, k, b):
                    dve.wait_ge(max_kept, s + 1)
                    nc.vector.tensor_scalar(old_max[:, k:k + 1], neg_max[:, bass.ds(b, 1)], 0.0, None, ALU.add).then_inc(max_read, 1)

                def add_sums(s1, k, b):
                    dve.wait_ge(summed, s1 + S)
                    dve.wait_ge(added, s1 + 1)
                    a = acc[:, bass.ds(b, 1), :]
                    nc.vector.scalar_tensor_tensor(out=a, in0=a, scalar=decay[:, k:k + 1], in1=banks[6 + k][:, 0:D1], op0=ALU.mult, op1=ALU.add).then_inc(added, 1)

                def window(i):
                    dve.load(regs, windows[bass.ds(i, 1), 0:U + 4])
                    return [dve.snap(r, min_val=0, max_val=B) for r in regs]

                blocks = window(0)
                dve.sem_inc(added, 1)
                dve.sem_inc(max_kept, 1)
                mark(0, 0, blocks[1])
                mark(0, 1, blocks[2])
                read_max(0, 0, blocks[1])
                edge_scores(0, 0, 0)
                dve.wait_ge(outside_done, 1)
                mark(0, 2, blocks[3])
                dve.wait_ge(sums_set, 1)
                with dve.Fori(0, n) as i:
                    blocks = window(i)
                    for u in range(U):
                        s, k = i * U + u, u % 2
                        step = dve.to_reg(s + 1)
                        dve.wait_ge(ones_set, 1)
                        dve.wait_ge(spread, step)
                        dve.wait_ge(outside_done, step)
                        dve.wait_ge(max_read, step)
                        nc.vector.tensor_tensor_reduce(out=masked, in0=banks[4][:], in1=outside[:, k, :], scale=-1.0, scalar=old_max[:, k:k + 1],
                                                       op0=ALU.add, op1=ALU.min, accum_out=new_max).then_inc(masked_done, 1)
                        edge_scores(i, u + 1, s + 1)
                        dve.wait_ge(masked_done, step)
                        nc.vector.tensor_scalar(neg_max[:, bass.ds(blocks[u + 1], 1)], new_max, 0.0, None, ALU.add).then_inc(max_kept, 1)
                        dve.wait_ge(outside_done, s + 2)
                        mark(i, u + 3, blocks[u + 4])
                        read_max(s + 1, 1 - k, blocks[u + 2])
                        add_sums(s, 1 - k, blocks[u])
                add_sums(n * U, 1, window(n)[0])

        used[0] = 0
        inv_sum = part(NB)
        weight_sum = part(NB)
        floor_sum = part(NB)
        u_rows = part(2 * D).rearrange("p (k n) -> p k n", k=2)
        u_T = part(2 * D).rearrange("p (k n) -> p k n", k=2)
        r_in = part(2 * D).rearrange("p (k n) -> p k n", k=2)
        y_mid = part(2 * D).rearrange("p (k n) -> p k n", k=2)
        y_rows = part(2 * D).rearrange("p (k n) -> p k n", k=2)
        y_scaled = part(2 * D).rearrange("p (k n) -> p k n", k=2)
        fT = part(2 * F).rearrange("p (k n) -> p k n", k=2)
        x_again = part(2 * D).rearrange("p (k n) -> p k n", k=2)
        o_rows = part(2 * D).rearrange("p (k n) -> p k n", k=2)

        inv_link, inv_done = sem("inv_link"), sem("inv_done")
        r_back = [sem(f"r_back{k}") for k in range(2)]
        u_done, uT_ready, uT_copied, o_ready, y_half, y_done = (sem(n) for n in ("u_done", "uT_ready", "uT_copied", "o_ready", "y_half", "y_done"))
        n_done, g_half, y_ready, yT_ready, yT_copied, ff1_ready, gelu_done, ff2_ready, z_half, z_done = (
            sem(n) for n in ("n_done", "g_half", "y_ready", "yT_ready", "yT_copied", "ff1_ready", "gelu_done", "ff2_ready", "z_half", "z_done"))
        x_back = [sem(f"x_back{k}") for k in range(2)]
        zn_done, zg_done, zb_done, o_done = (sem(n) for n in ("zn_done", "zg_done", "zb_done", "o_done"))
        o_stored = [sem(f"o_stored{k}") for k in range(2)]
        PAIRS = NB // 2

        with nc.Block() as block:
            @block.sync
            def _(sp):
                for k in range(2):
                    sp.dma_start(r_in[:, k, :], r_rows[k * P:(k + 1) * P, :]).then_inc(r_back[k], 16)
                with sp.Fori(1, PAIRS) as i:
                    for k in range(2):
                        sp.wait_ge(y_half, i * 2 + (k - 1))
                        sp.dma_start(r_in[:, k, :], r_rows[bass.ds((i * 2 + k) * P, P), :]).then_inc(r_back[k], 16)
                for k in range(2):
                    sp.dma_start(x_again[:, k, :], x[k * P:(k + 1) * P, :]).then_inc(x_back[k], 16)
                for k in range(2):
                    sp.wait_ge(o_done, k + 1)
                    sp.dma_start(out[k * P:(k + 1) * P, :], o_rows[:, k, :]).then_inc(o_stored[k], 16)
                    sp.dma_start(x_again[:, k, :], x[(2 + k) * P:(3 + k) * P, :]).then_inc(x_back[k], 16)
                with sp.Fori(1, FULL // 2 - 1) as i:
                    for k in range(2):
                        sp.wait_ge(o_done, i * 2 + (k + 1))
                        sp.dma_start(out[bass.ds((i * 2 + k) * P, P), :], o_rows[:, k, :]).then_inc(o_stored[k], 16)
                        sp.dma_start(x_again[:, k, :], x[bass.ds((i * 2 + k + 2) * P, P), :]).then_inc(x_back[k], 16)
                for k in range(2):
                    b = FULL - 2 + k
                    sp.wait_ge(o_done, b + 1)
                    sp.dma_start(out[b * P:(b + 1) * P, :], o_rows[:, k, :]).then_inc(o_stored[k], 16)
                    if k == 0:
                        sp.dma_start(x_again[0:REST, 0, :], x[FULL * P:N, :]).then_inc(x_back[0], 16)
                sp.wait_ge(o_done, FULL + 1)
                sp.dma_start(out[FULL * P:N, :], o_rows[0:REST, 0, :]).then_inc(o_stored[0], 16)
                sp.wait_ge(o_stored[0], 16 * (FULL // 2 + 1))
                sp.wait_ge(o_stored[1], 16 * (FULL // 2))

            @block.scalar
            def _(act):
                act.wait_ge(inv_done, 1)

                def scale_u(i, k):
                    nc.scalar.activation(u_rows[:, k, :], acc[:, bass.ds(i, 1), 0:D], ACT.Copy, scale=inv_sum[:, bass.ds(i, 1)]).then_inc(u_done, 1)

                scale_u(0, 0)
                scale_u(1, 1)
                with act.Fori(1, PAIRS) as i:
                    for k in range(2):
                        act.wait_ge(uT_ready, i * 2 + (k - 1))
                        act.wait_ge(inv_done, 1)
                        scale_u(i * 2 + k, k)
                act.wait_ge(var_done, 2)
                nc.scalar.activation(tmp[:], rstd[:], ACT.Sqrt, bias=eps[:, 0:1]).then_inc(std_done, 1)
                act.wait_ge(ln_done, 2)

                def normalise(i, k, sem_done):
                    nc.scalar.activation(u_rows[:, k, :], acc[:, bass.ds(i, 1), 0:D], ACT.Identity, bias=nmr[:, bass.ds(i, 1)], scale=rstd[:, bass.ds(i, 1)]).then_inc(sem_done, 1)

                def gelu(i, k):
                    act.wait_ge(ff1_ready, i + 1)
                    for c in range(FC):
                        last = nc.scalar.activation(fT[:, k, c * P:(c + 1) * P], banks[2 + k][:, c * P:(c + 1) * P], ACT.Gelu_apprx_tanh, bias=bff1_col[:, c:c + 1])
                    last.then_inc(gelu_done, 1)

                normalise(0, 0, n_done)
                normalise(1, 1, n_done)
                with act.Fori(1, PAIRS) as i:
                    for k in range(2):
                        gelu(i * 2 + (k - 2), k)
                        act.wait_ge(g_half, i * 2 + (k - 1))
                        act.wait_ge(inv_done, 1)
                        normalise(i * 2 + k, k, n_done)
                for k in range(2):
                    gelu(NB - 2 + k, k)
                act.wait_ge(var_done, 3)
                nc.scalar.activation(tmp[:], rstd[:], ACT.Sqrt, bias=eps[:, 0:1]).then_inc(std_done, 1)
                act.wait_ge(ln_done, 3)
                normalise(0, 0, zn_done)
                normalise(1, 1, zn_done)
                with act.Fori(1, FULL // 2) as i:
                    for k in range(2):
                        act.wait_ge(zg_done, i * 2 + (k - 1))
                        act.wait_ge(inv_done, 1)
                        normalise(i * 2 + k, k, zn_done)
                act.wait_ge(zg_done, FULL - 1)
                normalise(FULL, 0, zn_done)

            @block.gpsimd
            def _(pool):
                def scale_y(i, k):
                    pool.wait_ge(n_done, i + 1)
                    nc.gpsimd.tensor_tensor(y_scaled[:, k, :], u_rows[:, k, :], row_of["g1"], ALU.mult).then_inc(g_half, 1)
                    pool.wait_ge(g_half, i + 1)
                    nc.gpsimd.tensor_tensor(y_rows[:, k, :], y_scaled[:, k, :], row_of["b1"], ALU.add).then_inc(y_ready, 1)

                scale_y(0, 0)
                scale_y(1, 1)
                with pool.Fori(1, PAIRS) as i:
                    for k in range(2):
                        pool.wait_ge(z_half, i * 2 + (k - 1))
                        scale_y(i * 2 + k, k)

                def scale_z(i, k):
                    pool.wait_ge(zn_done, i + 1)
                    nc.gpsimd.tensor_tensor(y_scaled[:, k, :], u_rows[:, k, :], row_of["g2"], ALU.mult).then_inc(zg_done, 1)

                scale_z(0, 0)
                scale_z(1, 1)
                with pool.Fori(1, FULL // 2) as i:
                    for k in range(2):
                        pool.wait_ge(zb_done, i * 2 + (k - 1))
                        scale_z(i * 2 + k, k)
                pool.wait_ge(zb_done, FULL - 1)
                scale_z(FULL, 0)

            @block.vector
            def _(dve):
                nc.vector.tensor_scalar(floor_sum, acc[:, :, D], 1e-12, None, ALU.max).then_inc(inv_link, 1)
                dve.wait_ge(inv_link, 1)
                nc.vector.reciprocal(inv_sum, floor_sum).then_inc(inv_link, 1)
                dve.wait_ge(inv_link, 2)
                nc.vector.tensor_tensor(weight_sum, acc[:, :, D], inv_sum, ALU.mult).then_inc(inv_done, 1)
                dve.wait_ge(inv_done, 1)

                def copy_uT(i, k):
                    dve.wait_ge(uT_ready, i + 1)
                    nc.vector.tensor_copy(u_T[:, k, :], banks[k][:, 0:D]).then_inc(uT_copied, 1)

                def first_sum(i, k, n, more):
                    if more:
                        copy_uT(i + 1, 1 - k)
                    dve.wait_ge(r_back[k], n * 16 + 16)
                    nc.vector.scalar_tensor_tensor(out=y_mid[:, k, :], in0=row_of["bv"], scalar=weight_sum[:, bass.ds(i, 1)], in1=r_in[:, k, :],
                                                   op0=ALU.mult, op1=ALU.add).then_inc(y_half, 1)
                    dve.wait_ge(o_ready, i + 1)
                    dve.wait_ge(y_half, i + 1)
                    nc.vector.tensor_tensor(acc[:, bass.ds(i, 1), 0:D], y_mid[:, k, :], banks[2 + k][:, 0:D], ALU.add).then_inc(y_done, 1)
                    dve.wait_ge(y_done, i + 1)
                    dve.wait_ge(inv_done, 1)
                    return nc.vector.bn_stats(stats[:, bass.ds(i, 1), :], acc[:, bass.ds(i, 1), 0:D])

                copy_uT(0, 0)
                with dve.Fori(0, PAIRS - 1) as i:
                    for k in range(2):
                        first_sum(i * 2 + k, k, i, True)
                first_sum(NB - 2, 0, PAIRS - 1, True)
                first_sum(NB - 1, 1, PAIRS - 1, False).then_inc(stats_done, 1)
                layer_stats(dve, 1)

                def copy_yT(i, k):
                    dve.wait_ge(yT_ready, i + 1)
                    nc.vector.tensor_copy(u_T[:, k, :], banks[k][:, 0:D]).then_inc(yT_copied, 1)

                def second_sum(i, k, more):
                    if more:
                        copy_yT(i + 1, 1 - k)
                    dve.wait_ge(ff2_ready, i + 1)
                    nc.vector.tensor_tensor(y_mid[:, k, :], banks[4 + k][:, 0:D], y_rows[:, k, :], ALU.add).then_inc(z_half, 1)
                    dve.wait_ge(z_half, i + 1)
                    nc.vector.tensor_tensor(acc[:, bass.ds(i, 1), 0:D], y_mid[:, k, :], row_of["b_ff2"], ALU.add).then_inc(z_done, 1)
                    dve.wait_ge(z_done, i + 1)
                    dve.wait_ge(inv_done, 1)
                    return nc.vector.bn_stats(stats[:, bass.ds(i, 1), :], acc[:, bass.ds(i, 1), 0:D])

                copy_yT(0, 0)
                with dve.Fori(0, PAIRS - 1) as i:
                    for k in range(2):
                        second_sum(i * 2 + k, k, True)
                second_sum(NB - 2, 0, True)
                second_sum(NB - 1, 1, False).then_inc(stats_done, 1)
                layer_stats(dve, 2)

                def third_sum(i, k, n, rows):
                    dve.wait_ge(zg_done, i + 1)
                    nc.vector.tensor_tensor(y_mid[:, k, :], y_scaled[:, k, :], row_of["b2"], ALU.add).then_inc(zb_done, 1)
                    dve.wait_ge(x_back[k], n * 16 + 16)
                    dve.wait_ge(zb_done, i + 1)
                    nc.vector.tensor_tensor(o_rows[0:rows, k, :], y_mid[0:rows, k, :], x_again[0:rows, k, :], ALU.add).then_inc(o_done, 1)

                third_sum(0, 0, 0, P)
                third_sum(1, 1, 0, P)
                with dve.Fori(1, FULL // 2) as i:
                    for k in range(2):
                        dve.wait_ge(o_stored[k], i * 16)
                        third_sum(i * 2 + k, k, i, P)
                dve.wait_ge(o_stored[0], (FULL // 2) * 16)
                third_sum(FULL, 0, FULL // 2, REST)

            @block.tensor
            def _(pe):
                def transpose_u(i, k):
                    pe.wait_ge(u_done, i + 1)
                    for c in range(DC):
                        last = nc.tensor.transpose(banks[k][:, c * P:(c + 1) * P], u_rows[:, k, c * P:(c + 1) * P], ident[:])
                    last.then_inc(uT_ready, 1)

                def output(i, k, more):
                    if more:
                        transpose_u(i + 1, 1 - k)
                    pe.wait_ge(uT_copied, i + 1)
                    for c in range(DC):
                        last = nc.tensor.matmul(banks[2 + k][:, 0:D], u_T[:, k, c * P:(c + 1) * P], wv_sb[:, c, :], start=(c == 0), stop=(c == DC - 1))
                    last.then_inc(o_ready, 1)

                transpose_u(0, 0)
                output(0, 0, True)
                output(1, 1, True)
                with pe.Fori(1, PAIRS - 1) as i:
                    for k in range(2):
                        pe.wait_ge(y_done, i * 2 + (k - 1))
                        output(i * 2 + k, k, True)
                for k in range(2):
                    pe.wait_ge(y_done, NB - 3 + k)
                    output(NB - 2 + k, k, k == 0)

                def transpose_y(i, k):
                    pe.wait_ge(y_ready, i + 1)
                    for c in range(DC):
                        last = nc.tensor.transpose(banks[k][:, c * P:(c + 1) * P], y_rows[:, k, c * P:(c + 1) * P], ident[:])
                    last.then_inc(yT_ready, 1)

                def feed_forward(i, k):
                    pe.wait_ge(yT_copied, i + 1)
                    for m in range(FC):
                        for c in range(DC):
                            last = nc.tensor.matmul(banks[2 + k][:, m * P:(m + 1) * P], w1_sb[:, c, m * P:(m + 1) * P], u_T[:, k, c * P:(c + 1) * P], start=(c == 0), stop=(c == DC - 1))
                    last.then_inc(ff1_ready, 1)

                def contract(i, k):
                    pe.wait_ge(gelu_done, i + 1)
                    for m in range(FC):
                        last = nc.tensor.matmul(banks[4 + k][:, 0:D], fT[:, k, m * P:(m + 1) * P], w2_sb[:, m, :], start=(m == 0), stop=(m == FC - 1))
                    last.then_inc(ff2_ready, 1)

                transpose_y(0, 0)
                feed_forward(0, 0)
                transpose_y(1, 1)
                feed_forward(1, 1)
                contract(0, 0)
                transpose_y(2, 0)
                with pe.Fori(1, PAIRS - 1) as i:
                    for k in range(2):
                        feed_forward(i * 2 + k, k)
                        contract(i * 2 + (k - 1), 1 - k)
                        transpose_y(i * 2 + (k + 1), 1 - k)
                feed_forward(NB - 2, 0)
                contract(NB - 3, 1)
                transpose_y(NB - 1, 1)
                feed_forward(NB - 1, 1)
                contract(NB - 2, 0)
                contract(NB - 1, 1)


_INS = ["x", "src", "dst", "edge_weight"] + ["L0_gnn_" + n for n in (
    "wq", "bq", "wk", "bk", "wv", "bv", "ws", "bs", "we", "be", "g1", "b1", "g2", "b2", "w_ff1", "b_ff1", "w_ff2", "b_ff2")]


def build(nc, shapes):
    args = [nc.dram_tensor(f"in_{n}", s, d, kind="ExternalInput").ap() for n, s, d in shapes]
    out = nc.dram_tensor("out", shapes[0][1], F32, kind="ExternalOutput").ap()
    gnn_layer(nc, *args, out)


def kernel(**inputs):
    import numpy as np
    import concourse.bacc as bacc
    from concourse.bass_utils import run_bass_kernel_spmd

    nc = bacc.Bacc("TRN2", target_bir_lowering=False, num_devices=1)
    arrays = {n: np.ascontiguousarray(inputs[n]) for n in _INS}
    build(nc, [(n, arrays[n].shape, mybir.dt.from_np(arrays[n].dtype)) for n in _INS])
    r = run_bass_kernel_spmd(nc, [{f"in_{n}": a for n, a in arrays.items()}], core_ids=[0])
    return r.results[0]["out"]
```

```python
from contextlib import ExitStack

import concourse.bass as bass
from concourse import mybir

F32 = mybir.dt.float32
BF16 = mybir.dt.bfloat16
I32 = mybir.dt.int32
ALU = mybir.AluOpType
ACT = mybir.ActivationFunctionType
AX_X = mybir.AxisListType.X

P = 128
J = 4
C = P * J
U = 8
S = 4
WINDOW = 16
BIG = 1e30
NO_MAX = 5e29
PAD_DST = 32767
FIRST = 16 - S
EPS = 1e-5


def ceil_div(a, b):
    return -(-a // b)


def gnn_layer(nc, x, src, dst, edge_weight, wq, bq, wk, bk, wv, bv, ws, bs, we, be, g1, b1, g2, b2,
              w_ff1, b_ff1, w_ff2, b_ff2, out):
    N, D = x.shape
    E = src.shape[0]
    F = w_ff1.shape[1]
    DC, FC = D // P, F // P
    D1 = D + 1
    SCALE = float(D) ** -0.5
    FULL = N // P
    REST = N - FULL * P
    B = ceil_div(N, P)
    NB = B + 1
    T = ceil_div(E, C)
    EP = T * C
    assert D == 2 * P and REST > 0 and FULL % 4 == 0 and E % 16 == 0 and B * P < PAD_DST
    XG = FULL // 4
    XH = 2 * XG
    MEASURED = ceil_div(B - XH, 2)
    CHECKED = MEASURED + 1
    PLANNED = CHECKED + 17
    assert CHECKED <= XH - 3 and PLANNED < B
    PADDED = EP + C
    PAD = PADDED - E
    ALL_STEPS = ceil_div(T * B, U) * U
    SORTED_STEPS = ceil_div(T + B, U) * U
    HEAD = min(SORTED_STEPS + 8, T * B)
    TAIL = ALL_STEPS + WINDOW - T * B
    LEN = FIRST + ALL_STEPS + WINDOW
    TRIPS, SORTED_TRIPS = ALL_STEPS // U, SORTED_STEPS // U
    TG = ceil_div(T, P)
    assert HEAD <= min(2 * T, 500) and B < P and EP // P >= max(PAD, C)

    ctx = ExitStack()
    with ctx:
        def sb(name, shape, dt=F32):
            return ctx.enter_context(nc.sbuf_tensor(name, shape, dt))

        def sem(name):
            return ctx.enter_context(nc.semaphore(name))

        def dram(name, shape, dt=F32):
            return nc.dram_tensor(name, shape, dt).ap()

        h_rows = dram("h_rows", (B * P, D))
        r_rows = dram("r_rows", (B * P, D))
        src_pad = dram("src_pad", (1, PADDED), I32)
        dst_pad = dram("dst_pad", (1, PADDED), I32)
        ew_pad = dram("ew_pad", (1, PADDED))
        step_edge = dram("step_edge", (1, LEN), I32)
        step_block = dram("step_block", (1, LEN), I32)
        windows = dram("windows", (TRIPS + 1, WINDOW), I32)

        acc = sb("acc", [P, NB, D1])
        q3 = sb("q3", [P, NB, 3, D1 + 1], BF16)
        ident = sb("ident", [P, P])
        ones = sb("ones", [P, P])
        onesb = sb("onesb", [P, 1], BF16)
        wv_sb = sb("wv_sb", [P, DC, D])
        w1_sb = sb("w1_sb", [P, DC, F])
        w2_sb = sb("w2_sb", [P, FC, D])
        bias_names = ["bs", "bv", "g1", "b1", "g2", "b2", "b_ff2"]
        bias = sb("bias", [P, len(bias_names), D])
        row_of = {n: bias[:, k, :] for k, n in enumerate(bias_names)}
        bff1_col = sb("bff1_col", [P, FC])
        g1_col = sb("g1_col", [P, DC])
        b1_col = sb("b1_col", [P, DC])
        wb = sb("wb", [P, 2])
        stats = sb("stats", [P, NB, 6])
        mean = sb("mean", [P, NB])
        rstd = sb("rstd", [P, NB])
        nmr = sb("nmr", [P, NB])
        tmp = sb("tmp", [P, NB])
        eps = sb("eps", [P, 1])
        node = sb("node", [P, NB])
        neg_max = sb("neg_max", [P, NB])
        n_trips = sb("n_trips", [1, 1], I32)
        idx = sb("idx", [P, S, J], I32)
        ew = sb("ew", [P, S, J])
        dstb = sb("dstb", [P, S, C], I32)
        onehot = sb("onehot", [P, 2, J, P], BF16)
        WORK = 8420
        work = sb("work", [P, WORK])

        used = [0]

        def part(n, dt=F32):
            used[0] += n
            assert used[0] <= WORK, used
            a = work[:, used[0] - n:used[0]]
            return a if dt == F32 else a.bitcast(dt)

        banks = [ctx.enter_context(nc.psum_tensor(f"bank{k}", [P, 512], F32)) for k in range(8)]

        used[0] = 0
        halves = lambda n: part(n).rearrange("p (c n) -> p c n", c=DC)
        slots = lambda k, n: part(k * n).rearrange("p (k n) -> p k n", k=k)
        w_both = part(2 * DC * D)
        wq_sb, wk_sb = (w_both[:, k * DC * D:(k + 1) * DC * D].rearrange("p (c n) -> p c n", c=DC) for k in range(2))
        r_out = w_both.rearrange("p (k n) -> p k n", k=4)
        ws_sb, wqT, wkT, wqk = halves(DC * D), halves(DC * D), halves(DC * D1), halves(DC * D1)
        bq_col = part(DC)
        bias_hi, bias_mid = (part((D1 + 1) // 2, BF16) for _ in range(2))
        bias_rest = part(D1)
        q_bias3 = part((D1 + 1) // 2, BF16)
        s_bias3 = part((D1 + 1) // 2, BF16)
        onesb_rows = part(P // 2, BF16)
        h_now = slots(4, D)
        hT = slots(2, D)
        q_rest = slots(2, D1)
        srow = part(HEAD)
        sorted_e, sorted_b, all_t, all_b = (part(HEAD) for _ in range(4))
        spare = dstb[:].rearrange("p u n -> p (u n)")
        row_e, row_b = spare[:, 0:HEAD], spare[:, HEAD:2 * HEAD]
        in_block = spare[:, 2 * HEAD:3 * HEAD].bitcast(F32)
        tri = spare[:, 3 * HEAD:3 * HEAD + P].bitcast(F32)
        next_one = spare[:, 3 * HEAD + P:3 * HEAD + 2 * P].bitcast(F32)
        below_row = spare[:, 3 * HEAD + 2 * P:3 * HEAD + 3 * P].bitcast(F32)
        spare2 = onehot[:].rearrange("p k j n -> p (k j n)")
        block_ended = spare2[:, 0:HEAD]
        chunk_below = spare2[:, HEAD:HEAD + TG * P].rearrange("p (g b) -> p g b", g=TG)
        below_i, full_chunks_i, steps_i, fill_i = (part(1, I32) for _ in range(4))
        below, full_chunks, some_edges, start, start_edges, steps, first_step, end_step, shift_edges = (part(1) for _ in range(9))
        is_block = part(1, BF16)[:, 0:1]
        below_row_i = all_t[:, 0:P].bitcast(I32)
        ends_i = part(TG, I32)
        ends = part(TG)
        falls = part(1)
        is_sorted = part(1)
        trips_f = part(1)
        trips_i = part(1, I32)
        node_i = part(NB, I32)
        tail_t = part(TAIL, I32)
        tail_b = part(TAIL, I32)
        EDGES_P = EP // P
        early = sb("early", [P, 2 * EDGES_P], I32)
        dst_a, dst_b = early[:, 0:EDGES_P], early[:, EDGES_P:2 * EDGES_P]
        padding, zeros_i = dst_a[:, 0:PAD], dst_b[:, 0:PAD]
        edges_of_chunk = dst_b[:, 0:C]
        pair_t = sb("pair_t", [B, T], I32)
        pair_b = sb("pair_b", [B, T], I32)

        ident_set, consts = sem("ident_set"), sem("consts")
        x_in = [sem(f"x_in{k}") for k in range(4)]
        x_rest_in, x_zero = sem("x_rest_in"), sem("x_zero")
        w_in, biases_in, ws_in, late_in = sem("w_in"), sem("biases_in"), sem("ws_in"), sem("late_in")
        edges_in, check_in, ends_in = sem("edges_in"), sem("check_in"), sem("ends_in")
        wT_ready, wT_copied, wqk_ready, wqk_copied = sem("wT_ready"), sem("wT_copied"), sem("wqk_ready"), sem("wqk_copied")
        bias_link, biases_split = sem("bias_link"), sem("biases_split")
        stats_done, ln_link, var_done, std_done, ln_done = (sem(n) for n in ("stats_done", "ln_link", "var_done", "std_done", "ln_done"))
        h_done, hT_ready, hT_copied = sem("h_done"), sem("hT_ready"), sem("hT_copied")
        h_stored = [sem(f"h_stored{k}") for k in range(4)]
        q_ready, hi_done, rest_done, mid_done, lo_done = (sem(n) for n in ("q_ready", "hi_done", "rest_done", "mid_done", "lo_done"))
        hws_ready, r_done = sem("hws_ready"), sem("r_done")
        r_stored = [sem(f"r_stored{k}") for k in range(4)]
        pairs_set, pairs_out, windows_out = sem("pairs_set"), sem("pairs_out"), sem("windows_out")
        plan_consts, falls_done, ends_compared, chunks_counted, chunk_known, chunk_in, starts_known, ends_ready, steps_known, sums_known, marked, counts_ready, plan_done, heads_out = (
            sem(n) for n in ("plan_consts", "falls_done", "ends_compared", "chunks_counted", "chunk_known", "chunk_in", "starts_known", "ends_ready",
                             "steps_known", "sums_known", "marked", "counts_ready", "plan_done", "heads_out"))
        plan = sem("plan")
        counted, ended, summed_steps, total, bad = (banks[7][:, 504 + k:505 + k] for k in range(5))
        edge_of_step, block_of_step = banks[7][0:1, 0:HEAD], banks[6][0:1, 0:HEAD]

        def turn4(b, at):
            return b // 4 if isinstance(b, int) else (b - at % 4) // 4

        def columns(v, n):
            return v.rearrange("(c p) -> p c", p=P)

        def every(v):
            return v.rearrange("(a n) -> a n", a=1).to_broadcast((P, v.shape[0]))

        def step_windows(first, end):
            return bass.AP(tensor=step_block.tensor, offset=FIRST - 1 + first * U, ap=[[U, end - first], [1, WINDOW]])

        def layer_variance(dve, turn, first, end):
            blocks = slice(first, end)
            m, v, t = mean[:, blocks], rstd[:, blocks], tmp[:, blocks]
            dve.wait_ge(stats_done, turn + 1)
            nc.vector.tensor_tensor(m, stats[:, blocks, 1], stats[:, blocks, 4], ALU.add)
            nc.vector.tensor_tensor(v, stats[:, blocks, 2], stats[:, blocks, 5], ALU.add)
            nc.vector.tensor_tensor(t, stats[:, blocks, 1], stats[:, blocks, 4], ALU.subtract).then_inc(ln_link, 1)
            dve.wait_ge(ln_link, 5 * turn + 2)
            nc.vector.tensor_scalar(m, m, 0.5, None, ALU.mult)
            nc.vector.tensor_tensor(t, t, t, ALU.mult).then_inc(ln_link, 1)
            dve.wait_ge(ln_link, 5 * turn + 3)
            nc.vector.tensor_scalar(t, t, 0.25, None, ALU.mult).then_inc(ln_link, 1)
            dve.wait_ge(ln_link, 5 * turn + 4)
            nc.vector.scalar_tensor_tensor(out=v, in0=v, scalar=1.0 / D, in1=t, op0=ALU.mult, op1=ALU.add).then_inc(var_done, 1)

        def layer_deviation(act, turn, first, end):
            act.wait_ge(var_done, turn + 1)
            nc.scalar.activation(tmp[:, first:end], rstd[:, first:end], ACT.Sqrt, bias=eps[:, 0:1]).then_inc(std_done, 1)

        def layer_factors(dve, turn, first, end):
            blocks = slice(first, end)
            dve.wait_ge(std_done, turn + 1)
            nc.vector.reciprocal(rstd[:, blocks], tmp[:, blocks]).then_inc(ln_link, 1)
            dve.wait_ge(ln_link, 5 * turn + 5)
            nc.vector.scalar_tensor_tensor(out=nmr[:, blocks], in0=mean[:, blocks], scalar=-1.0, in1=rstd[:, blocks], op0=ALU.mult, op1=ALU.mult).then_inc(ln_link, 1)
            dve.wait_ge(ln_link, 5 * turn + 6)
            nc.vector.tensor_copy(tmp[:, blocks], nmr[:, blocks]).then_inc(ln_done, 1)

        def over(eng, first, end, step, body):
            turns = max(0, (end - first) // step)
            if turns:
                with eng.Fori(0, turns) as i:
                    for j in range(step):
                        body(i * step + (first + j), first + j)
            for b in range(first + turns * step, end):
                body(b, b)

        with nc.Block() as block:
            @block.sync
            def _(sp):
                for w, t in ((wq, wq_sb), (wk, wk_sb)):
                    sp.dma_start(t, w.rearrange("(c p) n -> p c n", p=P)).then_inc(w_in, 16)
                for k in range(4):
                    sp.dma_start(acc[:, k * XG:(k + 1) * XG, 0:D],
                                 x[k * XG * P:(k + 1) * XG * P, :].rearrange("(b p) d -> p b d", p=P)).then_inc(x_in[k], 16)
                sp.wait_ge(x_zero, 1)
                sp.dma_start(acc[0:REST, FULL, 0:D], x[FULL * P:N, :]).then_inc(x_rest_in, 16)
                for a, b in ((dst, dst_pad), (src, src_pad), (edge_weight, ew_pad)):
                    sp.dma_start(b[0, 0:E].rearrange("(a n) -> a n", a=16), a.rearrange("(a n) -> a n", a=16)).then_inc(edges_in, 16)
                sp.wait_ge(consts, 1)
                for a, b in ((zeros_i, src_pad), (padding, dst_pad)):
                    sp.dma_start(b[0:1, E:E + PAD], a[0:1, :]).then_inc(edges_in, 16)
                sp.dma_start(ew_pad[0:1, E:E + PAD], zeros_i[0:1, :].bitcast(F32)).then_inc(edges_in, 16)

                def store_h(b, at):
                    sp.wait_ge(h_done, b + 1)
                    sp.dma_start(h_rows[bass.ds(b * P, P), :], h_now[:, at % 4, :]).then_inc(h_stored[at % 4], 16)

                def store_r(b, at):
                    sp.wait_ge(r_done, b + 1)
                    sp.dma_start(r_rows[bass.ds(b * P, P), :], r_out[:, at % 4, :]).then_inc(r_stored[at % 4], 16)

                def store(b, at):
                    store_r(b - 1, at - 1)
                    store_h(b + 3, at + 3)

                for b in range(4):
                    store_h(b, b)
                over(sp, 1, B - 3, 4, store)
                for b in range(B - 4, B):
                    store_r(b, b)
                for k in range(4):
                    sp.wait_ge(h_stored[k], 16 * ceil_div(B - k, 4))
                    sp.wait_ge(r_stored[k], 16 * ceil_div(B - k, 4))
                sp.wait_ge(late_in, 16 * 14)

            @block.gpsimd
            def _(pool):
                pool.memset(ident[:], 0.0).then_inc(ident_set, 1)
                pool.wait_ge(ident_set, 1)
                pool.affine_select(out=ident[:], in_=ident[:], compare_op=ALU.not_equal, fill=1.0, base=0,
                                   pattern=[[-1, P]], channel_multiplier=1).then_inc(ident_set, 1)
                pool.memset(zeros_i[0:1, :], 0)
                pool.memset(padding[0:1, :], PAD_DST).then_inc(consts, 1)
                pool.memset(ends_i, PAD_DST).then_inc(consts, 1)
                pool.memset(tail_t[0:1, :], 0)
                pool.memset(tail_b[0:1, :], B)
                pool.iota(pair_t[:, :], [[C, T]], base=0, channel_multiplier=0)
                pool.iota(pair_b[:, :], [[0, T]], base=0, channel_multiplier=1).then_inc(pairs_set, 1)
                pool.iota(row_e, [[1, HEAD]], base=0, channel_multiplier=0)
                pool.iota(below_i, [[0, 1]], base=0, channel_multiplier=P)
                pool.iota(below_row_i, [[P, P]], base=0, channel_multiplier=0)
                pool.memset(tri, 1.0)
                pool.memset(next_one, 0.0)
                pool.memset(is_block, 1.0)
                pool.iota(node_i, [[P, NB]], base=0, channel_multiplier=1).then_inc(consts, 1)
                pool.wait_ge(pairs_set, 1)
                for tab, pairs, tail in ((step_edge, pair_t, tail_t), (step_block, pair_b, tail_b)):
                    pool.dma_start(tab[0, FIRST:FIRST + T * B].rearrange("(b t) -> b t", t=T), pairs[:, :]).then_inc(pairs_out, 16)
                    pool.dma_start(tab[0:1, FIRST + T * B:FIRST + T * B + TAIL], tail[0:1, :]).then_inc(pairs_out, 16)
                pool.dma_start(step_block[0:1, FIRST - 1:FIRST], tail_b[0:1, 0:1]).then_inc(pairs_out, 16)
                pool.memset(q3[:, B], 0.0)
                pool.wait_ge(edges_in, 6 * 16)
                pool.wait_ge(consts, 2)
                pool.dma_start(dst_a, dst_pad[0, 0:EP].rearrange("(p n) -> p n", p=P)).then_inc(check_in, 16)
                pool.dma_start(dst_b, dst_pad[0, 1:EP + 1].rearrange("(p n) -> p n", p=P)).then_inc(check_in, 16)
                chunks = dst_pad[0, 0:EP].rearrange("(t c) -> t c", c=C)
                for g in range(TG):
                    n = min(P, T - g * P)
                    pool.dma_start(ends_i[0:n, g:g + 1], chunks[g * P:g * P + n, C - 1:C], allow_slow_non_contiguous=True).then_inc(ends_in, 16)
                pool.wait_ge(pairs_out, 5 * 16)
                pool.dma_start(windows[SORTED_TRIPS + 1:TRIPS + 1, :], step_windows(SORTED_TRIPS + 1, TRIPS + 1)).then_inc(windows_out, 16)
                g = nc.gpsimd
                pool.wait_ge(consts, 3)
                g.tensor_copy(srow, row_e)
                g.tensor_copy(node[:], node_i)
                g.tensor_copy(below, below_i)
                pool.affine_select(out=tri, in_=tri, compare_op=ALU.is_ge, fill=0.0, base=0, pattern=[[1, P]], channel_multiplier=-1)
                pool.affine_select(out=next_one, in_=next_one, compare_op=ALU.not_equal, fill=1.0, base=-1, pattern=[[-1, P]], channel_multiplier=1)
                pool.affine_select(out=is_block, in_=is_block, compare_op=ALU.is_ge, fill=0.0, base=B - 1, pattern=[[0, 1]], channel_multiplier=-1)
                g.tensor_copy(below_row, below_row_i).then_inc(plan_consts, 1)
                pool.wait_ge(ends_in, TG * 16)
                g.tensor_copy(ends, ends_i).then_inc(plan_consts, 1)
                pool.wait_ge(plan_consts, 2)
                for k in range(TG):
                    last = g.tensor_scalar(chunk_below[:, k, :], below_row, ends[:, k:k + 1], None, ALU.is_gt)
                last.then_inc(ends_compared, 1)
                pool.wait_ge(falls_done, 1)
                pool.wait_ge(chunk_known, 1)
                pool.indirect_dma_start(edges_of_chunk, None, dst_pad[0, 0:EP].rearrange("(t c) -> t c", c=C),
                                        bass.IndirectOffsetOnAxis(full_chunks_i, 0)).then_inc(chunk_in, 16)

                def clear(first, end):
                    pool.wait_ge(h_done, min(end, B))
                    pool.memset(acc[:, first:end, :], 0.0)

                clear(0, XG)
                pool.wait_ge(plan_done, 1)
                pool.wait_ge(windows_out, 16)
                for tab, row in ((step_block, row_b), (step_edge, row_e)):
                    pool.dma_start(tab[0:1, FIRST:FIRST + HEAD], row[0:1, :]).then_inc(heads_out, 16)
                pool.wait_ge(heads_out, 2 * 16)
                pool.dma_start(windows[0:SORTED_TRIPS + 1, :], step_windows(0, SORTED_TRIPS + 1)).then_inc(windows_out, 16)
                for k in range(1, 4):
                    clear(k * XG, (k + 1) * XG)
                clear(FULL, NB)
                pool.wait_ge(windows_out, 2 * 16)

            @block.scalar
            def _(act):
                with nc.allow_non_contiguous_dma("columns of biases"):
                    act.dma_start(wkT[:, :, D], columns(bk, DC)).then_inc(biases_in, 16)
                    act.dma_start(bq_col, columns(bq, DC)).then_inc(biases_in, 16)
                    act.dma_start(row_of["bs"], every(bs)).then_inc(biases_in, 16)
                    act.dma_start(ws_sb, ws.rearrange("(c p) n -> p c n", p=P)).then_inc(ws_in, 16)
                    for t, v, n in ((bff1_col, b_ff1, FC), (g1_col, g1, DC), (b1_col, b1, DC)):
                        act.dma_start(t[:], columns(v, n)).then_inc(late_in, 16)
                for n, v in zip(bias_names[1:], (bv, g1, b1, g2, b2, b_ff2)):
                    act.dma_start(row_of[n], every(v)).then_inc(late_in, 16)
                act.dma_start(wb[:, 0:1], every(we.rearrange("a b -> (a b)"))).then_inc(late_in, 16)
                act.dma_start(wb[:, 1:2], every(be)).then_inc(late_in, 16)
                act.dma_start(wv_sb[:], wv.rearrange("(c p) n -> p c n", p=P)).then_inc(late_in, 16)
                act.dma_start(w1_sb[:], w_ff1.rearrange("(c p) n -> p c n", p=P)).then_inc(late_in, 16)
                act.dma_start(w2_sb[:], w_ff2.rearrange("(c p) n -> p c n", p=P)).then_inc(late_in, 16)

                def normalise(b, at):
                    if not (isinstance(b, int) and b < 4):
                        act.wait_ge(ln_done, 1)
                        act.wait_ge(r_done, b - 3)
                        act.wait_ge(h_stored[at % 4], turn4(b, at) * 16)
                    nc.scalar.activation(h_now[:, at % 4, :], acc[:, bass.ds(b, 1), 0:D], ACT.Relu, bias=nmr[:, bass.ds(b, 1)], scale=rstd[:, bass.ds(b, 1)]).then_inc(h_done, 1)

                def first_part(b, at):
                    act.wait_ge(ln_done, 1)
                    act.wait_ge(q_ready, b + 1)
                    nc.scalar.copy(q3[:, bass.ds(b, 1), 0, 0:D1], banks[2 + at % 2][:, 0:D1]).then_inc(hi_done, 1)

                def second_part(b, at):
                    act.wait_ge(ln_done, 1)
                    act.wait_ge(rest_done, b + 1)
                    nc.scalar.copy(q3[:, bass.ds(b, 1), 1, 0:D1], q_rest[:, at % 2, :]).then_inc(mid_done, 1)

                def split(b, at):
                    second_part(b - 1, at - 1)
                    first_part(b, at)
                    if not (isinstance(b, int) and b + 3 >= B):
                        normalise(b + 3, at + 3)

                layer_deviation(act, 0, 0, XH)
                act.wait_ge(ln_done, 1)
                for b in range(3):
                    normalise(b, b)
                first_part(0, 0)
                normalise(3, 3)
                over(act, 1, MEASURED + 1, 4, split)
                layer_deviation(act, 1, XH, B)
                over(act, MEASURED + 1, XH - 3, 4, split)
                act.wait_ge(ln_done, 2)
                over(act, XH - 3, B - 3, 4, split)
                for b in range(B - 3, B):
                    split(b, b)
                second_part(B - 1, B - 1)

            @block.vector
            def _(dve):
                nc.vector.memset(acc[:, FULL:NB, :], 0.0).then_inc(x_zero, 1)
                nc.vector.memset(eps[:], EPS)
                nc.vector.memset(ones[:], 1.0)
                nc.vector.memset(onesb[:], 1.0)
                nc.vector.memset(q_bias3, 0.0)
                nc.vector.memset(s_bias3, 0.0)
                nc.vector.memset(neg_max[:], NO_MAX).then_inc(ln_link, 1)
                for k in range(2 * DC):
                    dve.wait_ge(wT_ready, k + 1)
                    nc.vector.tensor_copy((wqT if k < DC else wkT)[:, k % DC, 0:D], banks[k][:, 0:D]).then_inc(wT_copied, 1)
                for k in range(2):
                    dve.wait_ge(x_in[k], 16)
                    for b in range(k * XG, (k + 1) * XG):
                        last = nc.vector.bn_stats(stats[:, b, :], acc[:, b, 0:D])
                last.then_inc(stats_done, 1)
                layer_variance(dve, 0, 0, XH)
                layer_factors(dve, 0, 0, XH)
                for k in range(DC):
                    dve.wait_ge(wqk_ready, k + 1)
                    nc.vector.tensor_copy(wqk[:, k, :], banks[4 + k][:, 0:D1]).then_inc(wqk_copied, 1)
                dve.wait_ge(wqk_ready, DC + 1)
                dve.wait_ge(biases_in, 3 * 16)
                link = 0
                for n, row, parts in ((D1, banks[6][:, 0:D1], q_bias3), (D, row_of["bs"], s_bias3)):
                    hi, mid, rest = bias_hi[:, 0:n], bias_mid[:, 0:n], bias_rest[:, 0:n]
                    nc.vector.tensor_copy(hi, row).then_inc(bias_link, 1)
                    dve.wait_ge(bias_link, link + 1)
                    nc.vector.tensor_tensor(rest, row, hi, ALU.subtract).then_inc(bias_link, 1)
                    dve.wait_ge(bias_link, link + 2)
                    nc.vector.tensor_copy(mid, rest).then_inc(bias_link, 1)
                    nc.vector.tensor_copy(parts[0:1, 0:n], hi[0:1, :])
                    dve.wait_ge(bias_link, link + 3)
                    nc.vector.tensor_copy(parts[32:33, 0:n], mid[32:33, :])
                    nc.vector.tensor_tensor(parts[64:65, 0:n], rest[64:65, :], mid[64:65, :], ALU.subtract).then_inc(bias_link, 1)
                    link += 4
                    dve.wait_ge(bias_link, link)
                nc.vector.tensor_copy(onesb_rows, ones[:]).then_inc(biases_split, 1)

                def copy_hT(b, at):
                    dve.wait_ge(hT_ready, b + 1)
                    nc.vector.tensor_copy(hT[:, at % 2, :], banks[at % 2][:, 0:D]).then_inc(hT_copied, 1)

                def third_part(b, at):
                    dve.wait_ge(mid_done, b + 1)
                    nc.vector.tensor_tensor(q3[:, bass.ds(b, 1), 2, 0:D1], q_rest[:, at % 2, :], q3[:, bass.ds(b, 1), 1, 0:D1], ALU.subtract).then_inc(lo_done, 1)

                def what_is_left(b, at):
                    if not (isinstance(b, int) and b < 2):
                        dve.wait_ge(lo_done, b - 1)
                    dve.wait_ge(hi_done, b + 1)
                    nc.vector.tensor_tensor(q_rest[:, at % 2, :], banks[2 + at % 2][:, 0:D1], q3[:, bass.ds(b, 1), 0, 0:D1], ALU.subtract).then_inc(rest_done, 1)

                def add_h(b, at):
                    if not (isinstance(b, int) and b < 4):
                        dve.wait_ge(r_stored[at % 4], turn4(b, at) * 16)
                    dve.wait_ge(hws_ready, b + 1)
                    nc.vector.tensor_tensor(r_out[:, at % 4, :], banks[4 + at % 2][:, 0:D], h_now[:, at % 4, :], ALU.add).then_inc(r_done, 1)

                def split(b, at):
                    if not (isinstance(b, int) and b + 1 >= B):
                        copy_hT(b + 1, at + 1)
                    if not (isinstance(b, int) and b == 0):
                        add_h(b - 1, at - 1)
                        third_part(b - 1, at - 1)
                    what_is_left(b, at)

                copy_hT(0, 0)
                dve.wait_ge(x_in[2], 16)
                dve.wait_ge(x_in[3], 16)
                dve.wait_ge(x_rest_in, 16)
                for b in range(MEASURED):
                    split(b, b)
                    for other in range(XH + 2 * b, min(XH + 2 * b + 2, B)):
                        last = nc.vector.bn_stats(stats[:, other, :], acc[:, other, 0:D])
                last.then_inc(stats_done, 1)
                layer_variance(dve, 1, XH, B)
                split(MEASURED, MEASURED)
                layer_factors(dve, 1, XH, B)
                dve.wait_ge(check_in, 32)
                nc.vector.tensor_tensor(dst_a, dst_a, dst_b, ALU.is_gt).then_inc(falls_done, 1)
                over(dve, CHECKED, CHECKED + 3, 4, split)
                dve.wait_ge(falls_done, 1)
                nc.vector.tensor_reduce(falls, dst_a, AX_X, ALU.add).then_inc(falls_done, 1)
                over(dve, CHECKED + 3, CHECKED + 5, 4, split)
                dve.wait_ge(chunks_counted, 1)
                nc.vector.tensor_scalar(full_chunks, counted, float(T - 1), None, ALU.min).then_inc(plan, 1)
                dve.wait_ge(plan, 1)
                nc.vector.tensor_copy(full_chunks_i, full_chunks).then_inc(chunk_known, 1)
                over(dve, CHECKED + 5, CHECKED + 8, 4, split)
                dve.wait_ge(chunk_in, 16)
                dve.wait_ge(plan_consts, 2)
                nc.vector.tensor_scalar(edges_of_chunk, edges_of_chunk, below, None, ALU.is_lt).then_inc(plan, 1)
                dve.wait_ge(plan, 2)
                nc.vector.tensor_reduce(some_edges, edges_of_chunk, AX_X, ALU.add).then_inc(plan, 1)
                dve.wait_ge(plan, 3)
                nc.vector.scalar_tensor_tensor(out=start, in0=full_chunks, scalar=float(C), in1=some_edges, op0=ALU.mult, op1=ALU.add).then_inc(starts_known, 1)
                over(dve, CHECKED + 8, CHECKED + 10, 4, split)
                dve.wait_ge(ends_ready, 1)
                nc.vector.scalar_tensor_tensor(out=fill_i, in0=ended, scalar=float(C - 1), in1=start, op0=ALU.add, op1=ALU.subtract).then_inc(plan, 1)
                dve.wait_ge(plan, 4)
                nc.vector.tensor_scalar(steps_i, fill_i, C.bit_length() - 1, None, ALU.arith_shift_right).then_inc(plan, 1)
                dve.wait_ge(plan, 5)
                nc.vector.tensor_copy(steps, steps_i).then_inc(plan, 1)
                dve.wait_ge(plan, 6)
                nc.vector.tensor_tensor(steps, steps, is_block, ALU.mult).then_inc(steps_known, 1)
                over(dve, CHECKED + 10, CHECKED + 12, 4, split)
                dve.wait_ge(sums_known, 1)
                nc.vector.tensor_copy(end_step, summed_steps)
                nc.vector.tensor_tensor(first_step, summed_steps, steps, ALU.subtract).then_inc(plan, 1)
                dve.wait_ge(plan, 7)
                nc.vector.scalar_tensor_tensor(out=shift_edges, in0=first_step, scalar=-float(C), in1=start, op0=ALU.mult, op1=ALU.add)
                nc.vector.tensor_scalar(block_ended, srow, end_step, None, ALU.is_ge).then_inc(plan, 1)
                dve.wait_ge(plan, 8)
                nc.vector.scalar_tensor_tensor(out=in_block, in0=srow, scalar=first_step, in1=block_ended, op0=ALU.is_ge, op1=ALU.subtract).then_inc(marked, 1)
                over(dve, CHECKED + 12, PLANNED, 4, split)
                dve.wait_ge(counts_ready, 1)
                nc.vector.tensor_scalar(is_sorted[0:1, :], bad[0:1], 0.0, None, ALU.is_equal)
                nc.vector.tensor_scalar(trips_i[0:1, :], total[0:1], float(U - 1), None, ALU.add)
                nc.vector.scalar_tensor_tensor(out=sorted_e[0:1, :], in0=srow[0:1, :], scalar=float(C), in1=edge_of_step, op0=ALU.mult, op1=ALU.add)
                nc.vector.tensor_scalar(all_b[0:1, :], srow[0:1, :], float(T), None, ALU.is_ge).then_inc(plan, 1)
                dve.wait_ge(plan, 9)
                nc.vector.tensor_scalar(trips_i[0:1, :], trips_i[0:1, :], U.bit_length() - 1, None, ALU.arith_shift_right)
                nc.vector.tensor_scalar(sorted_e[0:1, :], sorted_e[0:1, :], float(E - 1), None, ALU.min)
                nc.vector.tensor_tensor(sorted_b[0:1, :], block_of_step, all_b[0:1, :], ALU.subtract)
                nc.vector.scalar_tensor_tensor(out=all_t[0:1, :], in0=all_b[0:1, :], scalar=-float(T), in1=srow[0:1, :], op0=ALU.mult, op1=ALU.add).then_inc(plan, 1)
                dve.wait_ge(plan, 10)
                nc.vector.tensor_copy(trips_f[0:1, :], trips_i[0:1, :])
                nc.vector.tensor_scalar(all_t[0:1, :], all_t[0:1, :], float(C), None, ALU.mult)
                nc.vector.scalar_tensor_tensor(out=row_b[0:1, :], in0=sorted_b[0:1, :], scalar=is_sorted[0:1, 0:1], in1=all_b[0:1, :], op0=ALU.mult, op1=ALU.add).then_inc(plan, 1)
                dve.wait_ge(plan, 11)
                nc.vector.tensor_tensor(sorted_e[0:1, :], sorted_e[0:1, :], all_t[0:1, :], ALU.subtract)
                nc.vector.tensor_scalar(trips_f[0:1, :], trips_f[0:1, :], -float(TRIPS), is_sorted[0:1, 0:1], ALU.add, ALU.mult).then_inc(plan, 1)
                dve.wait_ge(plan, 12)
                nc.vector.tensor_scalar(n_trips[:], trips_f[0:1, :], float(TRIPS), None, ALU.add)
                nc.vector.scalar_tensor_tensor(out=row_e[0:1, :], in0=sorted_e[0:1, :], scalar=is_sorted[0:1, 0:1], in1=all_t[0:1, :], op0=ALU.mult, op1=ALU.add).then_inc(plan_done, 1)
                over(dve, PLANNED, B - 1, 4, split)
                split(B - 1, B - 1)
                add_h(B - 1, B - 1)
                third_part(B - 1, B - 1)

            @block.tensor
            def _(pe):
                pe.wait_ge(ident_set, 2)
                pe.wait_ge(w_in, 2 * 16)
                for k in range(2 * DC):
                    w = wq_sb if k < DC else wk_sb
                    c = k % DC
                    for r in range(DC):
                        last = nc.tensor.transpose(banks[k][:, r * P:(r + 1) * P], w[:, r, c * P:(c + 1) * P], ident[:])
                    last.then_inc(wT_ready, 1)
                pe.wait_ge(wT_copied, 2 * DC)
                pe.wait_ge(biases_in, 3 * 16)
                for r in range(DC):
                    for c in range(DC):
                        last = nc.tensor.matmul(banks[4 + r][:, 0:D1], wqT[:, c, r * P:(r + 1) * P], wkT[:, c, :], start=(c == 0), stop=(c == DC - 1))
                    last.then_inc(wqk_ready, 1)
                for c in range(DC):
                    last = nc.tensor.matmul(banks[6][:, 0:D1], bq_col[:, c:c + 1].broadcast_to([P, P]), wkT[:, c, :], start=(c == 0), stop=(c == DC - 1))
                last.then_inc(wqk_ready, 1)

                def transpose_h(b, at):
                    pe.wait_ge(h_done, b + 1)
                    for c in range(DC):
                        last = nc.tensor.transpose(banks[at % 2][:, c * P:(c + 1) * P], h_now[:, at % 4, c * P:(c + 1) * P], ident[:])
                    last.then_inc(hT_ready, 1)

                def project(b, at):
                    k = at % 2
                    pe.wait_ge(hT_copied, b + 1)
                    if not (isinstance(b, int) and b < 2):
                        pe.wait_ge(rest_done, b - 1)
                    nc.tensor.matmul(banks[2 + k][:, 0:D1], onesb_rows, q_bias3[:, 0:D1], start=True, stop=False)
                    for c in range(DC):
                        last = nc.tensor.matmul(banks[2 + k][:, 0:D1], hT[:, k, c * P:(c + 1) * P], wqk[:, c, :], start=False, stop=(c == DC - 1))
                    last.then_inc(q_ready, 1)
                    if not (isinstance(b, int) and b < 2):
                        pe.wait_ge(r_done, b - 1)
                    nc.tensor.matmul(banks[4 + k][:, 0:D], onesb_rows, s_bias3[:, 0:D], start=True, stop=False)
                    for c in range(DC):
                        last = nc.tensor.matmul(banks[4 + k][:, 0:D], hT[:, k, c * P:(c + 1) * P], ws_sb[:, c, :], start=False, stop=(c == DC - 1))
                    last.then_inc(hws_ready, 1)

                def turn_and_project(b, at):
                    transpose_h(b + 1, at + 1)
                    project(b, at)

                transpose_h(0, 0)
                pe.wait_ge(wqk_copied, DC)
                pe.wait_ge(biases_split, 1)
                pe.wait_ge(ws_in, 16)
                turn_and_project(0, 0)
                turn_and_project(1, 1)
                over(pe, 2, CHECKED + 4, 4, turn_and_project)
                pe.wait_ge(ends_compared, 1)
                for g in range(TG):
                    last = nc.tensor.matmul(counted, chunk_below[:, g, :], onesb[:], start=(g == 0), stop=(g == TG - 1))
                last.then_inc(chunks_counted, 1)
                over(pe, CHECKED + 4, CHECKED + 9, 4, turn_and_project)
                pe.wait_ge(starts_known, 1)
                nc.tensor.matmul(ended, next_one, start, start=True, stop=True).then_inc(ends_ready, 1)
                over(pe, CHECKED + 9, CHECKED + 11, 4, turn_and_project)
                pe.wait_ge(steps_known, 1)
                nc.tensor.matmul(summed_steps, tri, steps, start=True, stop=True)
                nc.tensor.matmul(total[0:1], steps, ones[:, 0:1], start=True, stop=True).then_inc(sums_known, 1)
                over(pe, CHECKED + 11, PLANNED - 1, 4, turn_and_project)
                pe.wait_ge(marked, 1)
                nc.tensor.matmul(block_of_step, is_block, block_ended, start=True, stop=True)
                nc.tensor.matmul(edge_of_step, shift_edges, in_block, start=True, stop=True)
                pe.wait_ge(falls_done, 2)
                nc.tensor.matmul(bad[0:1], falls, ones[:, 0:1], start=True, stop=True).then_inc(counts_ready, 1)
                over(pe, PLANNED - 1, B - 1, 4, turn_and_project)
                project(B - 1, B - 1)

        used[0] = 0
        rows = part(S * J * D1).rearrange("p (u j n) -> p u j n", u=S, j=J)
        masked = part(C)
        probsT = part(C)
        probs = part(C).rearrange("p (j n) -> p j n", j=J)
        outside = part(C, BF16)[:, 0:2 * C].rearrange("p (k n) -> p k n", k=2)
        product = part(J * (D1 + 1) // 2, BF16).rearrange("p (j n) -> p j n", j=J)
        score = part(2 * J).rearrange("p (k j) -> p k j", k=2)
        ew_term = part(2 * J).rearrange("p (k j) -> p k j", k=2)
        old_max = part(2)
        new_max = part(1)
        decay = part(2)

        ones_set, sums_set = sem("ones_set"), sem("sums_set")
        idx_in, ew_in, dst_in = ([sem(f"{n}{c}") for c in range(S)] for n in ("idx_in", "ew_in", "dst_in"))
        rows_in = [[sem(f"rows_in{u}_{j}") for j in range(J)] for u in range(U)]
        assert 16 * (TRIPS + 1) < 2 ** 16
        onehot_done, outside_done, q_edges, scored = sem("onehot_done"), sem("outside_done"), sem("q_edges"), sem("scored")
        ew_done, spread, max_read, masked_done, max_kept = (sem(n) for n in ("ew_done", "spread", "max_read", "masked_done", "max_kept"))
        exp_done, turned, probs_done, summed, added = (sem(n) for n in ("exp_done", "turned", "probs_done", "summed", "added"))

        def loaded(i, u):
            return i * (16 * (U // S)) + (u // S * 16 + 16)

        def gathered(i, u):
            return i * 16 + (u // U * 16 + 16)

        with nc.Block() as block:
            def trips(eng):
                return eng.value_load(n_trips[0:1, 0:1], min_val=ceil_div(T, U), max_val=TRIPS)

            @block.sync
            def _(sp):
                n = trips(sp)
                regs = [sp.alloc_register(f"first_edge{u}") for u in range(U)]

                def fetch(at, c):
                    sp.dma_start(idx[:, c, :], src_pad[0, bass.ds(at, C)].rearrange("(p j) -> p j", j=J)).then_inc(idx_in[c], 16)
                    sp.dma_start(dstb[:, c, :], dst_pad[0:1, bass.ds(at, C)].to_broadcast((P, C))).then_inc(dst_in[c], 16)
                    sp.dma_start(ew[:, c, :], ew_pad[0, bass.ds(at, C)].rearrange("(p j) -> p j", j=J)).then_inc(ew_in[c], 16)

                sp.load(regs[0:S], step_edge[0:1, FIRST:FIRST + S])
                for c in range(S):
                    fetch(sp.snap(regs[c], min_val=0, max_val=E - 1), c)
                with sp.Fori(0, n) as i:
                    sp.load(regs, step_edge[0:1, bass.ds(i * U + (FIRST + S), U)])
                    firsts = [sp.snap(r, min_val=0, max_val=E - 1) for r in regs]
                    for u in range(U):
                        used = sp.to_reg(i * (2 * U) + (2 * u + 2))
                        sp.wait_ge(edges_in, 6 * 16)
                        sp.wait_ge(scored, used)
                        fetch(firsts[u], u % S)
                last = sp.to_reg(loaded(n, 0))
                sp.wait_ge(edges_in, 6 * 16)
                for c in range(S):
                    for load in (idx_in[c], dst_in[c], ew_in[c]):
                        sp.wait_ge(load, last)

            @block.gpsimd
            def _(pool):
                n = trips(pool)

                def gather(i, u):
                    there, free = pool.to_reg(loaded(i, u)), pool.to_reg(i * U + (u + 1))
                    pool.wait_ge(windows_out, 2 * 16)
                    pool.wait_ge(summed, free)
                    pool.wait_ge(idx_in[u % S], there)
                    for j in range(J):
                        pool.indirect_dma_start(rows[:, u % S, j, 0:D], None, h_rows, bass.IndirectOffsetOnAxis(idx[:, u % S, j:j + 1], 0)).then_inc(rows_in[u][j], 16)

                with pool.Fori(0, n) as i:
                    for u in range(U):
                        gather(i, u)
                gather(n, 0)
                last = pool.to_reg(gathered(n, 0))
                for j in range(J):
                    pool.wait_ge(rows_in[0][j], last)

            @block.tensor
            def _(pe):
                n = trips(pe)
                regs = [pe.alloc_register(f"next_block{u}") for u in range(U)]

                def expand_q(k, half, b):
                    for j in (2 * half, 2 * half + 1):
                        for c in range(3):
                            last = nc.tensor.matmul(banks[j][:, 0:D1], onehot[:, k, j, :], q3[:, bass.ds(b, 1), c, 0:D1], start=(c == 0), stop=(c == 2))
                    last.then_inc(q_edges, 1)

                def spread_scores(k):
                    for j in range(J):
                        last = nc.tensor.transpose(banks[4][:, j * P:(j + 1) * P], score[:, k, j:j + 1].broadcast_to([P, P]), ident[:])
                    last.then_inc(spread, 1)

                pe.load(regs[0:2], windows[0:1, 1:3])
                first = [pe.snap(r, min_val=0, max_val=B) for r in regs[0:2]]
                pe.sem_inc(summed, S)
                pe.wait_ge(onehot_done, 1)
                expand_q(0, 0, first[0])
                expand_q(0, 1, first[0])
                pe.wait_ge(onehot_done, 2)
                pe.wait_ge(scored, 1)
                expand_q(1, 0, first[1])
                pe.wait_ge(scored, 2)
                spread_scores(0)
                expand_q(1, 1, first[1])
                with pe.Fori(0, n) as i:
                    pe.load(regs, windows[bass.ds(i, 1), 3:3 + U])
                    blocks = [pe.snap(r, min_val=0, max_val=B) for r in regs]
                    for u in range(U):
                        s, k = i * U + u, u % 2
                        pe.wait_ge(exp_done, s + 1)
                        for half in (1, 0):
                            for j in range(2):
                                last = nc.tensor.transpose(banks[5 - half][:, j * P:(j + 1) * P], probsT[:, (2 * half + j) * P:(2 * half + j + 1) * P], ident[:])
                            last.then_inc(turned, 1)
                        pe.wait_ge(onehot_done, s + 3)
                        pe.wait_ge(scored, s * 2 + 3)
                        expand_q(k, 0, blocks[u])
                        pe.wait_ge(scored, s * 2 + 4)
                        pe.wait_ge(probs_done, s * 2 + 1)
                        spread_scores(1 - k)
                        expand_q(k, 1, blocks[u])
                        for j in (2, 3, 0, 1):
                            if j == 0:
                                pe.wait_ge(probs_done, s * 2 + 2)
                            last = nc.tensor.matmul(banks[6 + k][:, 0:D1], probs[:, j, :], rows[:, u % S, j, :], start=(j == 2), stop=(j == 1))
                        last.then_inc(summed, 1)

            @block.scalar
            def _(act):
                n = trips(act)

                def prepare(i, u, s, k):
                    act.wait_ge(onehot_done, s + 1)
                    nc.scalar.activation(outside[:, k, :], onehot[:, k].rearrange("p j n -> p (j n)"), ACT.Copy, scale=BIG, bias=-BIG).then_inc(outside_done, 1)
                    act.wait_ge(ew_in[u % S], loaded(i, u))
                    nc.scalar.activation(ew_term[:, k, :], ew[:, u % S, :], ACT.Identity, bias=wb[:, 1:2], scale=wb[:, 0:1]).then_inc(ew_done, 1)

                nc.scalar.activation(decay[:, 1:2], eps[:, 0:1], ACT.Exp, scale=0.0).then_inc(sums_set, 1)
                prepare(0, 0, 0, 0)
                prepare(0, 1, 1, 1)
                with act.Fori(0, n) as i:
                    for u in range(U):
                        s, k = i * U + u, u % 2
                        act.wait_ge(masked_done, s + 1)
                        nc.scalar.activation(decay[:, k:k + 1], old_max[:, k:k + 1], ACT.Exp, bias=new_max, scale=-1.0)
                        nc.scalar.activation(probsT, masked, ACT.Exp, bias=new_max, scale=-1.0).then_inc(exp_done, 1)
                        for half in (1, 0):
                            act.wait_ge(turned, s * 2 + (2 - half))
                            nc.scalar.copy(probs[:, 2 * half:2 * half + 2, :].rearrange("p j n -> p (j n)"), banks[5 - half][:, 0:2 * P]).then_inc(probs_done, 1)
                        prepare(i, u + 2, s + 2, k)

            @block.vector
            def _(dve):
                n = trips(dve)
                regs = [dve.alloc_register(f"block{u}") for u in range(U + 4)]
                nc.vector.memset(rows[:, :, :, D:D1], 1.0).then_inc(ones_set, 1)
                nc.vector.memset(banks[7][:, 0:D1], 0.0).then_inc(sums_set, 1)

                def mark(i, u, b):
                    dve.wait_ge(dst_in[u % S], loaded(i, u))
                    nc.vector.tensor_scalar(onehot[:, u % 2], dstb[:, u % S, :].rearrange("p (n j) -> p j n", j=J), node[:, bass.ds(b, 1)], None, ALU.is_equal).then_inc(onehot_done, 1)

                def edge_scores(i, u, s):
                    there, first_half, second_half = dve.to_reg(gathered(i, u)), dve.to_reg(s * 2 + 1), dve.to_reg(s * 2 + 2)
                    dve.wait_ge(ones_set, 1)
                    dve.wait_ge(ew_done, s + 1)
                    for half, ready in ((0, first_half), (1, second_half)):
                        dve.wait_ge(ones_set, 1)
                        dve.wait_ge(q_edges, ready)
                        for j in (2 * half, 2 * half + 1):
                            dve.wait_ge(rows_in[u % U][j], there)
                        for j in (2 * half, 2 * half + 1):
                            last = nc.vector.tensor_tensor_reduce(out=product[:, j, 0:D1], in0=banks[j][:, 0:D1], in1=rows[:, u % S, j, :], scale=SCALE,
                                                                  scalar=ew_term[:, u % 2, j:j + 1], op0=ALU.mult, op1=ALU.add, accum_out=score[:, u % 2, j:j + 1])
                        last.then_inc(scored, 1)

                def read_max(s, k, b):
                    dve.wait_ge(max_kept, s + 1)
                    nc.vector.tensor_scalar(old_max[:, k:k + 1], neg_max[:, bass.ds(b, 1)], 0.0, None, ALU.add).then_inc(max_read, 1)

                def add_sums(s1, k, b):
                    dve.wait_ge(summed, s1 + S)
                    dve.wait_ge(added, s1 + 1)
                    a = acc[:, bass.ds(b, 1), :]
                    nc.vector.scalar_tensor_tensor(out=a, in0=a, scalar=decay[:, k:k + 1], in1=banks[6 + k][:, 0:D1], op0=ALU.mult, op1=ALU.add).then_inc(added, 1)

                def window(i):
                    dve.load(regs, windows[bass.ds(i, 1), 0:U + 4])
                    return [dve.snap(r, min_val=0, max_val=B) for r in regs]

                blocks = window(0)
                dve.sem_inc(added, 1)
                dve.sem_inc(max_kept, 1)
                mark(0, 0, blocks[1])
                mark(0, 1, blocks[2])
                read_max(0, 0, blocks[1])
                edge_scores(0, 0, 0)
                dve.wait_ge(outside_done, 1)
                mark(0, 2, blocks[3])
                dve.wait_ge(sums_set, 2)
                with dve.Fori(0, n) as i:
                    blocks = window(i)
                    for u in range(U):
                        s, k = i * U + u, u % 2
                        step = dve.to_reg(s + 1)
                        dve.wait_ge(ones_set, 1)
                        dve.wait_ge(spread, step)
                        dve.wait_ge(outside_done, step)
                        dve.wait_ge(max_read, step)
                        nc.vector.tensor_tensor_reduce(out=masked, in0=banks[4][:], in1=outside[:, k, :], scale=-1.0, scalar=old_max[:, k:k + 1],
                                                       op0=ALU.add, op1=ALU.min, accum_out=new_max).then_inc(masked_done, 1)
                        edge_scores(i, u + 1, s + 1)
                        dve.wait_ge(masked_done, step)
                        nc.vector.tensor_scalar(neg_max[:, bass.ds(blocks[u + 1], 1)], new_max, 0.0, None, ALU.add).then_inc(max_kept, 1)
                        dve.wait_ge(outside_done, s + 2)
                        mark(i, u + 3, blocks[u + 4])
                        read_max(s + 1, 1 - k, blocks[u + 2])
                        add_sums(s, 1 - k, blocks[u])
                add_sums(n * U, 1, window(n)[0])

        MIXED = (B - 1) // 6 * 2
        EARLY = 2 * MIXED
        used[0] = 0
        inv_sum = part(NB)
        weight_sum = part(NB)
        floor_sum = part(NB)
        b1_bff2 = part(D)
        r_in = slots(4, D)
        unit = slots(2, D)
        unit_T = slots(2, D)
        y_g1 = slots(2, D)
        y_rows = slots(2, D)
        fT = slots(2, F)
        x_again = slots(4, D)
        x_b2 = r_in
        z_unit = slots(4, D)
        r_bv = z_unit
        o_rows = slots(4, D)

        sums_inv, sums_ready = sem("sums_inv"), sem("sums_ready")
        r_back = [sem(f"r_back{k}") for k in range(4)]
        u_done, uT_ready, uT_copied, o_ready, r_bv_done, y_done = (sem(n) for n in ("u_done", "uT_ready", "uT_copied", "o_ready", "r_bv_done", "y_done"))
        unit_done, g1_done, y_ready, yT_ready, yT_copied, ff1_ready, gelu_done, ff2_ready, z_done = (
            sem(n) for n in ("unit_done", "g1_done", "y_ready", "yT_ready", "yT_copied", "ff1_ready", "gelu_done", "ff2_ready", "z_done"))
        b1_bff2_done = sem("b1_bff2_done")
        x_back = [sem(f"x_back{k}") for k in range(4)]
        z_unit_done, g2_done, x_b2_done, o_done = (sem(n) for n in ("z_unit_done", "g2_done", "x_b2_done", "o_done"))
        o_stored = [sem(f"o_stored{k}") for k in range(4)]

        def unit_slot(to, at):
            return to[:, at % (2 if to is unit else 4), :]

        def rows_of(at):
            return REST if at == B - 1 else P

        with nc.Block() as block:
            @block.sync
            def _(sp):
                def load_r(b, at):
                    sp.dma_start(r_in[:, at % 4, :], r_rows[bass.ds(b * P, P), :]).then_inc(r_back[at % 4], 16)

                for b in range(4):
                    load_r(b, b)
                for b in range(4):
                    sp.dma_start(x_again[:, b, :], x[b * P:(b + 1) * P, :]).then_inc(x_back[b], 16)

                def next_r(b, at):
                    sp.wait_ge(r_bv_done, b + 1)
                    load_r(b + 4, at)

                over(sp, 0, B - 4, 4, next_r)

                def store(b, at):
                    sp.wait_ge(o_done, b + 1)
                    sp.dma_start(out[bass.ds(b * P, rows_of(at)), :], o_rows[0:rows_of(at), at % 4, :]).then_inc(o_stored[at % 4], 16)

                def load_and_store(b, at):
                    sp.wait_ge(x_b2_done, b + 1)
                    sp.dma_start(x_again[:, at % 4, :], x[bass.ds((b + 4) * P, P), :]).then_inc(x_back[at % 4], 16)
                    store(b, at)

                over(sp, 0, B - 5, 4, load_and_store)
                sp.wait_ge(x_b2_done, B - 4)
                sp.dma_start(x_again[0:REST, (B - 1) % 4, :], x[FULL * P:N, :]).then_inc(x_back[(B - 1) % 4], 16)
                store(B - 5, B - 5)
                for b in range(B - 4, B):
                    store(b, b)
                for k in range(4):
                    sp.wait_ge(o_stored[k], 16 * ceil_div(B - k, 4))

            @block.scalar
            def _(act):
                act.wait_ge(sums_ready, 1)

                def weigh(b, at):
                    nc.scalar.activation(unit[:, at % 2, :], acc[:, bass.ds(b, 1), 0:D], ACT.Copy, scale=inv_sum[:, bass.ds(b, 1)]).then_inc(u_done, 1)

                def copy_uT(b, at):
                    act.wait_ge(uT_ready, b + 1)
                    nc.scalar.copy(unit_T[:, at % 2, :], banks[at % 2][:, 0:D]).then_inc(uT_copied, 1)

                weigh(0, 0)
                weigh(1, 1)

                def turn_and_weigh(b, at):
                    copy_uT(b, at)
                    act.wait_ge(sums_ready, 1)
                    weigh(b + 2, at)

                over(act, 0, B - 2, 2, turn_and_weigh)
                copy_uT(B - 2, B - 2)
                copy_uT(B - 1, B - 1)
                layer_deviation(act, 2, 0, B)
                act.wait_ge(ln_done, 3)

                def normalise(to, b, at):
                    return nc.scalar.activation(unit_slot(to, at), acc[:, bass.ds(b, 1), 0:D], ACT.Identity, bias=nmr[:, bass.ds(b, 1)], scale=rstd[:, bass.ds(b, 1)])

                def gelu(b, at):
                    act.wait_ge(ff1_ready, b + 1)
                    for c in range(FC):
                        last = nc.scalar.activation(fT[:, at % 2, c * P:(c + 1) * P], banks[2 + at % 2][:, c * P:(c + 1) * P], ACT.Gelu_apprx_tanh, bias=bff1_col[:, c:c + 1])
                    last.then_inc(gelu_done, 1)

                normalise(unit, 0, 0).then_inc(unit_done, 1)
                normalise(unit, 1, 1).then_inc(unit_done, 1)
                gelu(0, 0)
                act.wait_ge(g1_done, 1)
                normalise(unit, 2, 2).then_inc(unit_done, 1)

                def feed(b, at):
                    gelu(b + 1, at + 1)
                    act.wait_ge(g1_done, b + 2)
                    act.wait_ge(sums_ready, 1)
                    normalise(unit, b + 3, at + 3).then_inc(unit_done, 1)

                def last_unit(b, at):
                    if not (isinstance(b, int) and b < 4):
                        act.wait_ge(g2_done, b - 3)
                    act.wait_ge(sums_ready, 1)
                    normalise(z_unit, b, at).then_inc(z_unit_done, 1)

                over(act, 0, B - MIXED, 2, feed)
                layer_deviation(act, 3, 0, EARLY)
                act.wait_ge(ln_done, 4)
                for j in range(2):
                    last_unit(j, j)

                def mixed(i, j):
                    b, at = i * 2 + (B - MIXED + j), B - MIXED + j
                    if not (isinstance(i, int) and b + 1 >= B):
                        gelu(b + 1, at + 1)
                    if not (isinstance(i, int) and b + 3 >= B):
                        act.wait_ge(g1_done, b + 2)
                        act.wait_ge(sums_ready, 1)
                        normalise(unit, b + 3, at + 3).then_inc(unit_done, 1)
                    for c in range(2):
                        if not (isinstance(i, int) and i * 4 + (2 * j + c + 2) >= EARLY):
                            last_unit(i * 4 + (2 * j + c + 2), 2 * j + c + 2)

                for j in range(2):
                    mixed(0, j)
                if MIXED > 6:
                    with act.Fori(1, MIXED // 2 - 2) as i:
                        for j in range(2):
                            mixed(i, j)
                for i in range(max(1, MIXED // 2 - 2), MIXED // 2):
                    for j in range(2):
                        mixed(i, j)
                layer_deviation(act, 4, EARLY, B)
                act.wait_ge(ln_done, 5)
                over(act, EARLY, B, 4, last_unit)

            @block.gpsimd
            def _(pool):
                nc.gpsimd.tensor_tensor(b1_bff2, row_of["b1"], row_of["b_ff2"], ALU.add).then_inc(b1_bff2_done, 1)

                def scale_y(b, at):
                    k = at % 2
                    pool.wait_ge(unit_done, b + 1)
                    nc.gpsimd.tensor_tensor(y_g1[:, k, :], unit[:, k, :], row_of["g1"], ALU.mult).then_inc(g1_done, 1)
                    if not (isinstance(b, int) and b < 2):
                        pool.wait_ge(z_done, b - 1)
                    pool.wait_ge(g1_done, b + 1)
                    nc.gpsimd.tensor_tensor(y_rows[:, k, :], y_g1[:, k, :], b1_bff2, ALU.add).then_inc(y_ready, 1)

                def add_b2(b, at):
                    n = rows_of(at)
                    if not (isinstance(b, int) and b < 4):
                        pool.wait_ge(o_done, b - 3)
                    pool.wait_ge(x_back[at % 4], turn4(b, at) * 16 + 16)
                    nc.gpsimd.tensor_tensor(x_b2[0:n, at % 4, :], x_again[0:n, at % 4, :], row_of["b2"][0:n], ALU.add).then_inc(x_b2_done, 1)

                pool.wait_ge(b1_bff2_done, 1)
                scale_y(0, 0)
                scale_y(1, 1)
                over(pool, 2, B - MIXED, 2, scale_y)
                for j in range(2):
                    scale_y(B - MIXED + j, B - MIXED + j)
                    for c in range(2):
                        add_b2(2 * j + c, 2 * j + c)
                if MIXED > 2:
                    with pool.Fori(1, MIXED // 2) as i:
                        for j in range(2):
                            scale_y(i * 2 + (B - MIXED + j), B - MIXED + j)
                            for c in range(2):
                                add_b2(i * 4 + (2 * j + c), 2 * j + c)
                over(pool, EARLY, B - 1, 4, add_b2)
                add_b2(B - 1, B - 1)

            @block.vector
            def _(dve):
                nc.vector.tensor_scalar(floor_sum, acc[:, :, D], 1e-12, None, ALU.max).then_inc(sums_inv, 1)
                dve.wait_ge(sums_inv, 1)
                nc.vector.reciprocal(inv_sum, floor_sum).then_inc(sums_inv, 1)
                dve.wait_ge(sums_inv, 2)
                nc.vector.tensor_tensor(weight_sum, acc[:, :, D], inv_sum, ALU.mult).then_inc(sums_ready, 1)
                dve.wait_ge(sums_ready, 1)

                def add_bv(b, at):
                    dve.wait_ge(r_back[at % 4], turn4(b, at) * 16 + 16)
                    nc.vector.scalar_tensor_tensor(out=r_bv[:, at % 4, :], in0=row_of["bv"], scalar=weight_sum[:, bass.ds(b, 1)], in1=r_in[:, at % 4, :],
                                                   op0=ALU.mult, op1=ALU.add).then_inc(r_bv_done, 1)

                def add_output(b, at):
                    dve.wait_ge(o_ready, b + 1)
                    dve.wait_ge(r_bv_done, b + 1)
                    nc.vector.tensor_tensor(acc[:, bass.ds(b, 1), 0:D], r_bv[:, at % 4, :], banks[2 + at % 2][:, 0:D], ALU.add).then_inc(y_done, 1)

                def measure(b, done):
                    dve.wait_ge(done, b + 1)
                    dve.wait_ge(sums_ready, 1)
                    return nc.vector.bn_stats(stats[:, bass.ds(b, 1), :], acc[:, bass.ds(b, 1), 0:D])

                for b in range(3):
                    add_bv(b, b)
                add_output(0, 0)

                def first_sum(b, at):
                    add_bv(b + 2, at + 2)
                    add_output(b, at)
                    measure(b - 1, y_done)

                over(dve, 1, B - 2, 4, first_sum)
                for b in range(B - 2, B):
                    add_output(b, b)
                    measure(b - 1, y_done)
                measure(B - 1, y_done).then_inc(stats_done, 1)
                layer_variance(dve, 2, 0, B)
                layer_factors(dve, 2, 0, B)

                def copy_yT(b, at):
                    dve.wait_ge(yT_ready, b + 1)
                    for c in range(DC):
                        last = nc.vector.tensor_scalar(unit_T[:, at % 2, c * P:(c + 1) * P], banks[at % 2][:, c * P:(c + 1) * P], g1_col[:, c:c + 1], b1_col[:, c:c + 1], ALU.mult, ALU.add)
                    last.then_inc(yT_copied, 1)

                def second_sum(b, at):
                    dve.wait_ge(ff2_ready, b + 1)
                    dve.wait_ge(y_ready, b + 1)
                    nc.vector.tensor_tensor(acc[:, bass.ds(b, 1), 0:D], banks[4 + at % 2][:, 0:D], y_rows[:, at % 2, :], ALU.add).then_inc(z_done, 1)
                    return measure(b, z_done)

                def feed(b, at):
                    copy_yT(b + 2, at + 2)
                    return second_sum(b, at)

                def scale_z(b, at):
                    n = rows_of(at)
                    if not (isinstance(b, int) and b < 4):
                        dve.wait_ge(o_stored[at % 4], turn4(b, at) * 16)
                    dve.wait_ge(z_unit_done, b + 1)
                    nc.vector.tensor_tensor(o_rows[0:n, at % 4, :], z_unit[0:n, at % 4, :], row_of["g2"][0:n], ALU.mult).then_inc(g2_done, 1)

                def add_x(b, at):
                    n = rows_of(at)
                    dve.wait_ge(x_b2_done, b + 1)
                    dve.wait_ge(g2_done, b + 1)
                    nc.vector.tensor_tensor(o_rows[0:n, at % 4, :], o_rows[0:n, at % 4, :], x_b2[0:n, at % 4, :], ALU.add).then_inc(o_done, 1)

                copy_yT(0, 0)
                copy_yT(1, 1)
                over(dve, 0, EARLY - 1, 2, feed)
                feed(EARLY - 1, EARLY - 1).then_inc(stats_done, 1)
                layer_variance(dve, 3, 0, EARLY)
                for b in range(EARLY, B - MIXED):
                    feed(b, b)
                layer_factors(dve, 3, 0, EARLY)

                def mixed(i, j):
                    b, at = i * 2 + (B - MIXED + j), B - MIXED + j
                    if not (isinstance(i, int) and b + 2 >= B):
                        copy_yT(b + 2, at + 2)
                    last = second_sum(b, at)
                    if isinstance(i, int) and b == B - 1:
                        last.then_inc(stats_done, 1)
                    for step in (scale_z, add_x):
                        for c in range(2):
                            step(i * 4 + (2 * j + c), 2 * j + c)

                mixed(0, 0)
                mixed(0, 1)
                if MIXED > 4:
                    with dve.Fori(1, MIXED // 2 - 1) as i:
                        for j in range(2):
                            mixed(i, j)
                if MIXED > 2:
                    for j in range(2):
                        mixed(MIXED // 2 - 1, j)
                layer_variance(dve, 4, EARLY, B)
                layer_factors(dve, 4, EARLY, B)
                scale_z(EARLY, EARLY)

                def third_sum(b, at):
                    scale_z(b + 1, at + 1)
                    add_x(b, at)

                over(dve, EARLY, B - 2, 4, third_sum)
                third_sum(B - 2, B - 2)
                add_x(B - 1, B - 1)

            @block.tensor
            def _(pe):
                def transpose(b, at, rows_ready, turned):
                    pe.wait_ge(rows_ready, b + 1)
                    for c in range(DC):
                        last = nc.tensor.transpose(banks[at % 2][:, c * P:(c + 1) * P], unit[:, at % 2, c * P:(c + 1) * P], ident[:])
                    last.then_inc(turned, 1)

                def output(b, at):
                    if not (isinstance(b, int) and b < 2):
                        pe.wait_ge(y_done, b - 1)
                    pe.wait_ge(uT_copied, b + 1)
                    for c in range(DC):
                        last = nc.tensor.matmul(banks[2 + at % 2][:, 0:D], unit_T[:, at % 2, c * P:(c + 1) * P], wv_sb[:, c, :], start=(c == 0), stop=(c == DC - 1))
                    last.then_inc(o_ready, 1)

                def turn_and_output(b, at):
                    transpose(b + 1, at + 1, u_done, uT_ready)
                    output(b, at)

                transpose(0, 0, u_done, uT_ready)
                turn_and_output(0, 0)
                turn_and_output(1, 1)
                over(pe, 2, B - 1, 2, turn_and_output)
                output(B - 1, B - 1)

                def feed_forward(b, at):
                    pe.wait_ge(yT_copied, b + 1)
                    for m in range(FC):
                        for c in range(DC):
                            last = nc.tensor.matmul(banks[2 + at % 2][:, m * P:(m + 1) * P], w1_sb[:, c, m * P:(m + 1) * P], unit_T[:, at % 2, c * P:(c + 1) * P], start=(c == 0), stop=(c == DC - 1))
                    last.then_inc(ff1_ready, 1)

                def contract(b, at):
                    if not (isinstance(b, int) and b < 2):
                        pe.wait_ge(z_done, b - 1)
                    pe.wait_ge(gelu_done, b + 1)
                    for m in range(FC):
                        last = nc.tensor.matmul(banks[4 + at % 2][:, 0:D], fT[:, at % 2, m * P:(m + 1) * P], w2_sb[:, m, :], start=(m == 0), stop=(m == FC - 1))
                    last.then_inc(ff2_ready, 1)

                def feed(b, at):
                    transpose(b + 2, at + 2, unit_done, yT_ready)
                    feed_forward(b + 1, at + 1)
                    contract(b, at)

                transpose(0, 0, unit_done, yT_ready)
                transpose(1, 1, unit_done, yT_ready)
                feed_forward(0, 0)
                feed(0, 0)
                feed(1, 1)
                over(pe, 2, B - 2, 2, feed)
                feed_forward(B - 1, B - 1)
                contract(B - 2, B - 2)
                contract(B - 1, B - 1)


_INS = ["x", "src", "dst", "edge_weight"] + ["L0_gnn_" + n for n in (
    "wq", "bq", "wk", "bk", "wv", "bv", "ws", "bs", "we", "be", "g1", "b1", "g2", "b2", "w_ff1", "b_ff1", "w_ff2", "b_ff2")]


def build(nc, shapes):
    args = [nc.dram_tensor(f"in_{n}", s, d, kind="ExternalInput").ap() for n, s, d in shapes]
    out = nc.dram_tensor("out", shapes[0][1], F32, kind="ExternalOutput").ap()
    gnn_layer(nc, *args, out)


def kernel(**inputs):
    import numpy as np
    import concourse.bacc as bacc
    from concourse.bass_utils import run_bass_kernel_spmd

    nc = bacc.Bacc("TRN2", target_bir_lowering=False, num_devices=1)
    arrays = {n: np.ascontiguousarray(inputs[n]) for n in _INS}
    build(nc, [(n, arrays[n].shape, mybir.dt.from_np(arrays[n].dtype)) for n in _INS])
    r = run_bass_kernel_spmd(nc, [{f"in_{n}": a for n, a in arrays.items()}], core_ids=[0])
    return r.results[0]["out"]
```
